# Optimizing a Trainium2 kernel written in Bass

```python
import numpy as np
import jax
import jax.numpy as jnp

def _softmax(x, axis=-1):
    return jax.nn.softmax(x, axis=axis)
def _gelu(x):
    return jax.nn.gelu(x, approximate=True)
def _silu(x):
    return jax.nn.silu(x)
def _sigmoid(x):
    return jax.nn.sigmoid(x)
def _layernorm(x, axis=-1, eps=1e-5):
    m = jnp.mean(x, axis=axis, keepdims=True)
    v = jnp.var(x, axis=axis, keepdims=True)
    return (x - m) / jnp.sqrt(v + eps)
def _scatter_add(tgt, idx, src, axis=0):
    return tgt.at[idx].add(src)
def _segment_sum(src, seg, n):
    return jax.ops.segment_sum(src, seg, n)

kernel_name = 'mk_conv_preact_d2_conv_nhwc256_b8566f'

def setup_inputs(seed: int = 0):
    np.random.seed(seed)
    _w = jnp.asarray
    def _rec_inputs():
        import jax
        import jax.numpy as jnp
        _gk = jax.random.key(seed)
        x = 7.22e-05 + 1 * jax.random.normal(jax.random.fold_in(_gk, 1), (1, 128, 256, 256), jnp.float32)
        return x
    x = _rec_inputs()
    def _L0_conv_setup():
        import jax, jax.numpy as jnp
        import numpy as np
        import math
        ATTN_C = 32
        HEADS = 8
        IN_C = 256
        PAIR_C = 128
        B, M, N = (1, 128, 256)

        def _layernorm(x, w, b, eps=1e-05):
            mu = jnp.mean(x, axis=-1, keepdims=True)
            xc = x - mu
            var = jnp.mean(xc * xc, axis=-1, keepdims=True)
            return xc * jax.lax.rsqrt(var + eps) * w + b
        key = jax.random.key(seed)
        ks = jax.random.split(key, 10)
        s1 = 1.0 / math.sqrt(IN_C)
        s2 = 1.0 / math.sqrt(PAIR_C)
        s3 = 1.0 / math.sqrt(ATTN_C * HEADS)
        return {'x1d': jax.random.normal(ks[0], (B, M, N, IN_C), jnp.float32), 'x2d': jax.random.normal(ks[1], (B, N, N, PAIR_C), jnp.float32), 'norm_w': jnp.ones((IN_C,), jnp.float32), 'norm_b': jnp.zeros((IN_C,), jnp.float32), 'qkv_w': jax.random.normal(ks[2], (3 * ATTN_C * HEADS, IN_C), jnp.float32) * s1, 'x2d_w': jax.random.normal(ks[3], (HEADS, PAIR_C), jnp.float32) * s2, 'gate_w': jax.random.normal(ks[4], (ATTN_C * HEADS, IN_C), jnp.float32) * s1, 'gate_b': jnp.zeros((ATTN_C * HEADS,), jnp.float32), 'final_w': jax.random.normal(ks[5], (IN_C, ATTN_C * HEADS), jnp.float32) * s3, 'final_b': jnp.zeros((IN_C,), jnp.float32)}
    _L0_conv_all = _L0_conv_setup()
    _L0_conv_in = {k: v for k, v in _L0_conv_all.items() if k in ('x2d', 'norm_w', 'norm_b', 'qkv_w', 'x2d_w', 'gate_w', 'gate_b', 'final_w', 'final_b', )}
    del _L0_conv_all

    def _L1_conv_setup():
        import jax, jax.numpy as jnp
        import numpy as np
        NUM_HEADS = 4
        key = jax.random.key(seed)
        ks = jax.random.split(key, 5)
        B, T, F, C = (2, 128, 256, 256)
        s = 1.0 / np.sqrt(C)
        return {'x': jax.random.normal(ks[0], (B, T, F, C), jnp.float32), 'w_in': jax.random.normal(ks[1], (3 * C, C), jnp.float32) * s, 'b_in': jax.random.normal(ks[2], (3 * C,), jnp.float32) * 0.01, 'w_out': jax.random.normal(ks[3], (C, C), jnp.float32) * s, 'b_out': jax.random.normal(ks[4], (C,), jnp.float32) * 0.01, 'band': 16}
    _L1_conv_all = _L1_conv_setup()
    _L1_conv_in = {k: v for k, v in _L1_conv_all.items() if k in ('w_in', 'b_in', 'w_out', 'b_out', )}
    del _L1_conv_all

    return {
        "x": x,
        "L0_conv_x2d": _L0_conv_in["x2d"],
        "L0_conv_norm_w": _L0_conv_in["norm_w"],
        "L0_conv_norm_b": _L0_conv_in["norm_b"],
        "L0_conv_qkv_w": _L0_conv_in["qkv_w"],
        "L0_conv_x2d_w": _L0_conv_in["x2d_w"],
        "L0_conv_gate_w": _L0_conv_in["gate_w"],
        "L0_conv_gate_b": _L0_conv_in["gate_b"],
        "L0_conv_final_w": _L0_conv_in["final_w"],
        "L0_conv_final_b": _L0_conv_in["final_b"],
        "L1_conv_w_in": _L1_conv_in["w_in"],
        "L1_conv_b_in": _L1_conv_in["b_in"],
        "L1_conv_w_out": _L1_conv_in["w_out"],
        "L1_conv_b_out": _L1_conv_in["b_out"],
    }

def reference(x, L0_conv_x2d, L0_conv_norm_w, L0_conv_norm_b, L0_conv_qkv_w, L0_conv_x2d_w, L0_conv_gate_w, L0_conv_gate_b, L0_conv_final_w, L0_conv_final_b, L1_conv_w_in, L1_conv_b_in, L1_conv_w_out, L1_conv_b_out):
    import jax
    import jax.numpy as jnp
    def _L0_conv_ref(x1d, x2d, norm_w, norm_b, qkv_w, x2d_w, gate_w, gate_b, final_w, final_b):
        import jax, jax.numpy as jnp
        import numpy as np
        import math
        ATTN_C = 32
        HEADS = 8
        IN_C = 256
        PAIR_C = 128
        B, M, N = (1, 128, 256)

        def _layernorm(x, w, b, eps=1e-05):
            mu = jnp.mean(x, axis=-1, keepdims=True)
            xc = x - mu
            var = jnp.mean(xc * xc, axis=-1, keepdims=True)
            return xc * jax.lax.rsqrt(var + eps) * w + b
        c, h = (ATTN_C, HEADS)
        x = _layernorm(x1d, norm_w, norm_b)
        qkv = (x @ qkv_w.T).reshape(*x.shape[:-1], c, 3 * h)
        q, k, v = (qkv[..., :h], qkv[..., h:2 * h], qkv[..., 2 * h:])
        aff = jnp.einsum('bmich,bmjch->bmijh', q, k)
        gate = jax.nn.sigmoid(x @ gate_w.T + gate_b).reshape(*x.shape[:-1], c, h)
        factor = 1.0 / math.sqrt(c)
        bias = x2d @ x2d_w.T * factor
        weights = jax.nn.softmax(aff + bias[:, None], axis=-2)
        out = jnp.einsum('bmrch,bmirh->bmich', v, weights) * gate
        out = out.reshape(*x.shape[:-1], c * h) @ final_w.T + final_b
        return out

    def _L1_conv_ref(x, w_in, b_in, w_out, b_out, band):
        import jax, jax.numpy as jnp
        import numpy as np
        NUM_HEADS = 4
        B, T, F, C = x.shape
        H = NUM_HEADS
        D = C // H
        x2 = x.reshape(B * T, F, C)
        qkv = x2 @ w_in.T + b_in
        q, k, v = jnp.split(qkv, 3, axis=-1)

        def heads(t):
            return t.reshape(B * T, F, H, D).transpose(0, 2, 1, 3)
        q, k, v = (heads(q), heads(k), heads(v))
        scores = jnp.einsum('bhid,bhjd->bhij', q, k) / jnp.sqrt(jnp.asarray(D, x.dtype))
        i = jnp.arange(F)[:, None]
        j = jnp.arange(F)[None, :]
        keep = jnp.abs(i - j) <= band
        scores = jnp.where(keep, scores, -jnp.inf)
        attn = jax.nn.softmax(scores, axis=-1)
        out = jnp.einsum('bhij,bhjd->bhid', attn, v)
        out = out.transpose(0, 2, 1, 3).reshape(B * T, F, C)
        y = out @ w_out.T + b_out
        return y.reshape(B, T, F, C)

    def _gn(v, G=32, eps=1e-5):
        B_, H_, W_, C_ = v.shape
        g = v.reshape(B_, H_, W_, G, C_ // G)
        m = jnp.mean(g, axis=(1, 2, 4), keepdims=True)
        s = jnp.var(g, axis=(1, 2, 4), keepdims=True)
        return ((g - m) / jnp.sqrt(s + eps)).reshape(v.shape)

    def _ln_c(v, eps=1e-6):
        m = jnp.mean(v, axis=-1, keepdims=True)
        s = jnp.var(v, axis=-1, keepdims=True)
        return (v - m) / jnp.sqrt(s + eps)

    def _ln_t(v, eps=1e-5):
        m = jnp.mean(v, axis=-1, keepdims=True)
        s = jnp.var(v, axis=-1, keepdims=True)
        return (v - m) / jnp.sqrt(s + eps)

    def _to_tokens(v):
        B_, H_, W_, C_ = v.shape
        return v.reshape(B_, H_ * W_, C_)
    def _from_tokens(t, like):
        return t.reshape(like.shape)

    x = x + _L0_conv_ref(_gn(x), L0_conv_x2d, L0_conv_norm_w, L0_conv_norm_b, L0_conv_qkv_w, L0_conv_x2d_w, L0_conv_gate_w, L0_conv_gate_b, L0_conv_final_w, L0_conv_final_b)
    x = x + _L1_conv_ref(_gn(x), L1_conv_w_in, L1_conv_b_in, L1_conv_w_out, L1_conv_b_out, 16)
    return x


_drawn_inputs = setup_inputs


def setup_inputs(seed=0):
    import zlib

    import numpy as np

    out = dict(_drawn_inputs(seed))
    spreads = {'L0_conv_norm_w': (1.0, 0.2),
     'L0_conv_norm_b': (0.0, 0.1),
     'L0_conv_gate_b': (0.0, 0.477),
     'L0_conv_final_b': (0.0, 0.1)}
    factors = {'L1_conv_b_in': 5.357, 'L1_conv_b_out': 6.643}
    for name, (base, spread) in spreads.items():
        noise = np.random.default_rng([zlib.crc32(name.encode()), seed]).standard_normal(out[name].shape)
        drawn = base * np.exp(spread * noise) if base else spread * noise
        out[name] = jnp.asarray(drawn.astype(out[name].dtype))
    for name, factor in factors.items():
        out[name] = (out[name] * factor).astype(out[name].dtype)
    return out
```

```python
from contextlib import ExitStack

import numpy as np

import concourse.bass as bass
from concourse import mybir

F32 = mybir.dt.float32
ALU = mybir.AluOpType
ACT = mybir.ActivationFunctionType

P = 128
ROWS, TOK, CH = 128, 256, 256
CB = CH // P
TB = TOK // P
GROUP = CH // 32
EPS = 1e-5

H0, D0 = 8, 32
HG = H0 * D0 // P
HPG = P // D0
STEPS0 = H0 // 2
PAIR = 128

H1, D1 = 4, 64
HP = H1 // 2
BAND = 16
HALO = 32
WIN = P + HALO
FAR = 1.0e30

UNROLL = 4
XSLOTS = 4

XCHUNK = 2048
JCHUNK = 16


class Row:

    def __init__(self, loop, base):
        self.loop, self.base = loop, base

    def __add__(self, n):
        return Row(self.loop, self.base + n)

    @property
    def exists(self):
        return self.loop is not None or 0 <= self.base < ROWS

    def times(self, per, plus=0, of=1):
        fixed = per * (self.base // of) + plus
        return fixed if self.loop is None else self.loop * (per * UNROLL // of) + fixed

    def tokens(self):
        return bass.ds(self.times(TOK), TOK)


def wait(eng, sem, value):
    if isinstance(value, int):
        if value > 0:
            eng.wait_ge(sem, value)
    else:
        eng.wait_ge(sem, value)


def over_rows(eng, before, after, body):
    for m in range(-before, UNROLL):
        body(Row(None, m))
    with eng.Fori(0, ROWS // UNROLL - 2) as i:
        for k in range(UNROLL):
            body(Row(i, UNROLL + k))
    for m in range(ROWS - UNROLL, ROWS + after):
        body(Row(None, m))


def over_chunks(eng, count, body):
    body(lambda per, fixed: fixed)
    with eng.Fori(0, count // 2 - 1) as i:
        body(lambda per, fixed: i * per + (per + fixed))


def conv_preact_kernel(nc, xT, pairT, w0, wf0, pair_w, vec0, w1, wf1, vec1, bv1, ident_d, group_d, band_d, x1T, outT):
    x_v = xT.rearrange("(c p) t -> p c t", p=P)
    x1_v = x1T.rearrange("(c p) t -> p c t", p=P)
    out_v = outT.rearrange("(c p) t -> p c t", p=P)

    with ExitStack() as ctx:
        def sb(name, shape, dt=F32):
            return ctx.enter_context(nc.sbuf_tensor(name, shape, dt))

        def sem(name):
            return ctx.enter_context(nc.semaphore(name))

        ident = sb("ident", [P, P])
        group_mean = sb("group_mean", [P, P])
        band = sb("band", [P, TB, WIN])
        w0_sb = sb("w0_sb", [P, CB, 4 * CH])
        wf0_sb = sb("wf0_sb", [P, CB, CH])
        pairw_sb = sb("pairw_sb", [P, H0])
        vec0_sb = sb("vec0_sb", [P, 4, CB])
        w1_sb = sb("w1_sb", [P, CB, 3 * CH])
        wf1_sb = sb("wf1_sb", [P, CB, CH])
        vec1_sb = sb("vec1_sb", [P, 3, CB])
        bv1_sb = sb("bv1_sb", [P, CH])
        minus_half = sb("minus_half", [P, CB])
        half_gate_b = sb("half_gate_b", [P, CB])
        gstat0 = sb("gstat0", [P, CB, ROWS * TOK // 512, 6])
        gstat1 = sb("gstat1", [P, CB, ROWS, 6])
        ch_mv = sb("ch_mv", [P, CB, 2])
        gn_mean = sb("gn_mean", [P, CB])
        gn_dev = sb("gn_dev", [P, CB])
        gn_sq = sb("gn_sq", [P, CB])
        gn_var = sb("gn_var", [P, CB])
        gn_scale = [sb(f"gn_scale{n}", [P, CB]) for n in range(2)]
        gn_shift = [sb(f"gn_shift{n}", [P, CB]) for n in range(2)]
        x_chunk = sb("x_chunk", [P, 2, CB, XCHUNK])
        pair_chunk = sb("pair_chunk", [P, 2, JCHUNK, TOK])
        neg_bias = sb("neg_bias", [P, TB, H0, TOK])
        x_sb = sb("x_sb", [P, XSLOTS, CB, TOK])
        g_sb = sb("g_sb", [P, 2, CB, TOK])
        ln_st = sb("ln_st", [P, TB, 6])
        ln_mv = sb("ln_mv", [P, TB, 2])
        ln_var = sb("ln_var", [P, TB])
        ln_rstd = sb("ln_rstd", [P, TB])
        xn = sb("xn", [P, TB, CH])
        xnT = sb("xnT", [P, 2, CB, TOK])
        nqT = sb("nqT", [P, 2, CB, TOK])
        kT = sb("kT", [P, 2, CB, TOK])
        v_sb = sb("v_sb", [P, 4, TB, CH])
        gate = sb("gate", [P, 2, HG, TOK])
        prob = sb("prob", [P, STEPS0, 2, TB, TOK])
        row_min = sb("row_min", [P, STEPS0, 2, TB])
        row_sum = sb("row_sum", [P, STEPS0, 2, TB])
        row_inv = sb("row_inv", [P, STEPS0, 2, TB])
        probT = sb("probT", [P, 2, 2, TB, TOK])
        att = sb("att", [P, HG, TOK])
        y_sb = sb("y_sb", [P, 2, CB, TOK])
        prob1 = sb("prob1", [P, 2, HP, 2, TB, TOK])
        row_min1 = sb("row_min1", [P, 2, HP, 2, TB])
        row_sum1 = sb("row_sum1", [P, 2, HP, 2, TB])
        row_inv1 = sb("row_inv1", [P, 2, HP, 2, TB])
        probT1 = sb("probT1", [P, 2, 2, 2 * WIN])

        score = ctx.enter_context(nc.psum_tensor("score", [P, 4, TB, TOK], F32))
        turn = ctx.enter_context(nc.psum_tensor("turn", [P, 2 * TOK], F32))
        mix = ctx.enter_context(nc.psum_tensor("mix", [P, 2, TOK], F32))
        work = ctx.enter_context(nc.psum_tensor("work", [P, 2, 2, TOK], F32))

        consts_in = sem("consts_in")
        consts_set = sem("consts_set")
        wf0_halved = sem("wf0_halved")
        x_chunk_in = [sem(f"x_chunk_in{n}") for n in range(2)]
        x_chunk_used = sem("x_chunk_used")
        pair_in = [sem(f"pair_in{n}") for n in range(2)]
        bias_ps = sem("bias_ps")
        bias_done = sem("bias_done")
        gn_chain = [sem(f"gn_chain{n}") for n in range(2)]
        gn_ps = [sem(f"gn_ps{n}") for n in range(2)]
        gn_rstd = [sem(f"gn_rstd{n}") for n in range(2)]
        gn_ready = [sem(f"gn_ready{n}") for n in range(2)]

        x_in = [[sem(f"x_in{n}_{s}") for s in range(XSLOTS)] for n in range(2)]
        g_done = [sem(f"g_done{n}") for n in range(2)]
        t1_done = sem("t1_done")
        ln_chain = sem("ln_chain")
        ln_var_done = sem("ln_var_done")
        ln_rstd_done = sem("ln_rstd_done")
        xn_done = sem("xn_done")
        t2_done = sem("t2_done")
        xnT_done = sem("xnT_done")
        q_ps = [sem(f"q_ps{n}") for n in range(2)]
        k_ps = [sem(f"k_ps{n}") for n in range(2)]
        v_ps = [sem(f"v_ps{n}") for n in range(2)]
        gate_ps = sem("gate_ps")
        y_ps = [sem(f"y_ps{n}") for n in range(2)]
        q_done = [sem(f"q_done{n}") for n in range(2)]
        k_done = [sem(f"k_done{n}") for n in range(2)]
        v_done = [sem(f"v_done{n}") for n in range(2)]
        gate_done = sem("gate_done")
        y_done = [sem(f"y_done{n}") for n in range(2)]
        y_stats = sem("y_stats")
        score_done = [sem(f"score_done{n}") for n in range(2)]
        min_done = [sem(f"min_done{n}") for n in range(2)]
        exp_done = [sem(f"exp_done{n}") for n in range(2)]
        inv_done = [sem(f"inv_done{n}") for n in range(2)]
        norm_done = [sem(f"norm_done{n}") for n in range(2)]
        turn_ps = [[sem(f"turn_ps{n}_{a}") for a in range(2)] for n in range(2)]
        turn_done = [[sem(f"turn_done{n}_{a}") for a in range(2)] for n in range(2)]
        halo_ps = sem("halo_ps")
        mix_ps = [sem(f"mix_ps{n}") for n in range(2)]
        att_done = [sem(f"att_done{n}") for n in range(2)]
        prob1_clear = sem("prob1_clear")
        y_out = [[sem(f"y_out{n}_{s}") for s in range(2)] for n in range(2)]

        NXC = ROWS * TOK // XCHUNK
        NJC = TOK // JCHUNK

        pool_passed, act_passed, dve_passed, sp_passed, pe_passed = (
            sem(f"{e}_passed") for e in ("pool", "act", "dve", "sp", "pe"))

        def apart(eng, passed):
            eng.sem_inc(passed, 1)

        block = ctx.enter_context(nc.Block())

        @block.sync
        def _(sp):
            for dst, src in ((ident, ident_d), (group_mean, group_d), (band, band_d), (w0_sb, w0), (wf0_sb, wf0),
                             (pairw_sb, pair_w), (vec0_sb, vec0), (w1_sb, w1), (wf1_sb, wf1), (vec1_sb, vec1)):
                sp.dma_start(dst[:], src).then_inc(consts_in, 16)
            sp.dma_start(bv1_sb[:], bv1.broadcast_to([P, CH])).then_inc(consts_in, 16)

            def chunks(plus):
                for b in range(2):
                    wait(sp, x_chunk_used, plus(16, 8 * b - 8))
                    apart(sp, sp_passed)
                    sp.dma_start(x_chunk[:, b], x_v[:, :, bass.ds(plus(2 * XCHUNK, b * XCHUNK), XCHUNK)]
                                 ).then_inc(x_chunk_in[b], 16)
                    wait(sp, bias_ps, plus(4, 2 * b - 2))
                    apart(sp, sp_passed)
                    sp.dma_start(pair_chunk[:, b], pairT[:, bass.ds(plus(2 * JCHUNK, b * JCHUNK), JCHUNK), :]
                                 ).then_inc(pair_in[b], 16)

            over_chunks(sp, NXC, chunks)

            def rows(n, src, dst):
                def body(m):
                    if (m + -1).exists:
                        wait(sp, y_done[n], m.times(CB))
                        apart(sp, sp_passed)
                        sp.dma_start(dst[:, :, (m + -1).tokens()], y_sb[:, (m.base - 1) % 2]
                                     ).then_inc(y_out[n][(m.base - 1) % 2], 16)
                    if (m + 3).exists and (m.loop is not None or m.base + 3 < ROWS):
                        slot = (m.base + 3) % XSLOTS
                        sp.dma_start(x_sb[:, slot], src[:, :, (m + 3).tokens()]).then_inc(x_in[n][slot], 16)

                over_rows(sp, 3, 1, body)
                for s in range(2):
                    sp.wait_ge(y_out[n][s], 16 * ROWS // 2)

            rows(0, x_v, x1_v)
            rows(1, x1_v, out_v)

        @block.gpsimd
        def _(pool):
            pool.memset(minus_half[:], -0.5).then_inc(consts_set, 1)

            def power(n):
                pool.wait_ge(consts_set, 2)
                pool.wait_ge(gn_chain[n], 7)
                pool.tensor_tensor(gn_scale[n][:], gn_var[:], minus_half[:], ALU.pow).then_inc(gn_rstd[n], 1)
                pool.wait_ge(gn_ready[n], 1)

            def affine(n, m, waits):
                wait(pool, x_in[n][m.base % XSLOTS], m.times(16, 16, of=XSLOTS))
                waits()
                apart(pool, pool_passed)
                for cb in range(CB):
                    ins = pool.tensor_scalar(g_sb[:, m.base % 2, cb], x_sb[:, m.base % XSLOTS, cb],
                                             gn_scale[n][:, cb:cb + 1], gn_shift[n][:, cb:cb + 1], ALU.mult, ALU.add)
                ins.then_inc(g_done[n], 1)

            power(0)

            def body0(m):
                for s in range(STEPS0):
                    r, g = (m, s + 1) if s + 1 < STEPS0 else (m + 1, 0)
                    if r.exists:
                        wait(pool, inv_done[0], r.times(STEPS0, g + 1))
                        apart(pool, pool_passed)
                        for a in range(2):
                            for ib in range(TB):
                                pool.tensor_scalar(prob[:, g, a, ib], prob[:, g, a, ib], row_inv[:, g, a, ib:ib + 1],
                                                   1.0, ALU.mult, ALU.mult).then_inc(norm_done[0], 1)
                    if s == 0 and (m + 2).exists:
                        affine(0, m + 2, lambda: wait(pool, t1_done, (m + 2).times(1, -1)))
                    if s == 2 and (m + 2).exists:
                        wait(pool, ln_var_done, (m + 2).times(1, 1))
                        apart(pool, pool_passed)
                        pool.tensor_tensor(ln_rstd[:], ln_var[:], minus_half[:], ALU.pow).then_inc(ln_rstd_done, 1)

            over_rows(pool, 2, 0, body0)

            pool.memset(prob1[:], 0.0).then_inc(prob1_clear, 1)
            power(1)

            def body1(m):
                for s in range(HP):
                    r, g = (m, 1) if s == 0 else (m + 1, 0)
                    if r.exists:
                        wait(pool, inv_done[1], r.times(HP, g + 1))
                        apart(pool, pool_passed)
                        for a in range(2):
                            for ib in range(TB):
                                w = prob1[:, r.base % 2, g, a, ib, ib * (TOK - WIN):ib * (TOK - WIN) + WIN]
                                pool.tensor_scalar(w, w, row_inv1[:, r.base % 2, g, a, ib:ib + 1], 1.0,
                                                   ALU.mult, ALU.mult).then_inc(norm_done[1], 1)
                    if s == 1 and (m + 3).exists:
                        affine(1, m + 3, lambda: wait(pool, v_ps[1], (m + 3).times(1, -1)))

            over_rows(pool, 3, 0, body1)

        @block.tensor
        def _(pe):
            pe.wait_ge(consts_in, 16 * 11)
            def pair_bias(plus):
                for b in range(2):
                    wait(pe, pair_in[b], plus(16, 16))
                    wait(pe, bias_done, plus(4, 2 * b - 2))
                    for ib in range(TB):
                        for j in range(JCHUNK):
                            ins = pe.matmul(score[:, 2 * b + ib, 0, j * H0:(j + 1) * H0],
                                            pair_chunk[:, b, j, ib * P:(ib + 1) * P], pairw_sb[:],
                                            start=True, stop=True)
                        ins.then_inc(bias_ps, 1)

            over_chunks(pe, NJC, pair_bias)

            def group_sums(n):
                pe.wait_ge(gn_chain[n], 2)
                pe.matmul(mix[:, 0, 0:CB], group_mean[:], ch_mv[:, :, 0], start=True, stop=True).then_inc(gn_ps[n], 1)
                pe.wait_ge(gn_chain[n], 6)
                pe.matmul(mix[:, 0, CB:2 * CB], group_mean[:], gn_sq[:], start=True, stop=True).then_inc(gn_ps[n], 1)

            group_sums(0)
            pe.wait_ge(wf0_halved, 1)

            def project(out, w, cols, src):
                for cb in range(CB):
                    for kb in range(CB):
                        ins = pe.matmul(out[:, cb], w[:, kb, cols + cb * P:cols + (cb + 1) * P], src[:, kb],
                                        start=kb == 0, stop=kb == CB - 1)
                return ins

            def project_tokens(out, w, cols, src):
                for tb in range(TB):
                    for kb in range(CB):
                        ins = pe.matmul(out[:, tb], src[:, kb, tb * P:(tb + 1) * P], w[:, kb, cols:cols + CH],
                                        start=kb == 0, stop=kb == CB - 1)
                return ins

            def body0(m):
                last, nxt, far = m + -1, m + 1, m + 2
                src = xnT[:, nxt.base % 2]

                def scores(r, g):
                    wait(pe, q_done[0], r.times(1, 1))
                    wait(pe, k_done[0], r.times(1, 1))
                    wait(pe, min_done[0], r.times(4 * STEPS0, 4 * (g - 1)))
                    for ib in range(TB):
                        for a in range(2):
                            hg, h = divmod(2 * g + a, HPG)
                            q = slice(h * D0, (h + 1) * D0)
                            ins = pe.matmul(score[:, h, ib], nqT[q, r.base % 2, hg, ib * P:(ib + 1) * P],
                                            kT[q, r.base % 2, hg], start=True, stop=True)
                            if ib == TB - 1:
                                ins.then_inc(score_done[0], 1)

                def turns(g, a):
                    wait(pe, norm_done[0], m.times(4 * STEPS0, 4 * g + 2 * (a + 1)))
                    if a == 0:
                        wait(pe, turn_done[0][1], m.times(STEPS0, g))
                    else:
                        wait(pe, turn_done[0][0], m.times(STEPS0, g + 1))
                    for jb in range(TB):
                        for ib in range(TB):
                            ins = pe.transpose(turn[:, jb * TOK + ib * P:jb * TOK + (ib + 1) * P],
                                               prob[:, g, a, ib, jb * P:(jb + 1) * P], ident[:])
                    ins.then_inc(turn_ps[0][a], 1)

                def mixes(g):
                    wait(pe, v_done[0], m.times(1, 1))
                    wait(pe, att_done[0], m.times(1, 0))
                    for a in range(2):
                        wait(pe, turn_done[0][a], m.times(STEPS0, g + 1))
                    for jb in range(TB):
                        for a in range(2):
                            hg, h = divmod(2 * g + a, HPG)
                            c = (2 * g + a) * D0
                            ins = pe.matmul(mix[h * D0:(h + 1) * D0, hg], v_sb[:, m.base % 2, jb, c:c + D0],
                                            probT[:, g % 2, a, jb], start=jb == 0, stop=jb == TB - 1,
                                            skip_group_check=True)
                    ins.then_inc(mix_ps[0], 1)

                def task(s, n):
                    if (s, n) == (0, 0) and nxt.exists:
                        wait(pe, xnT_done, nxt.times(CB, CB))
                        project(work[:, 0], w0_sb, 0, src).then_inc(q_ps[0], 1)
                    if (s, n) == (0, 1) and nxt.exists:
                        wait(pe, gate_done, m.times(HG, HG))
                        project(work[:, 1], w0_sb, CH, src).then_inc(k_ps[0], 1)
                    if (s, n) == (1, 0) and nxt.exists:
                        wait(pe, q_done[0], nxt.times(1, 1))
                        project_tokens(work[:, 0], w0_sb, 2 * CH, src).then_inc(v_ps[0], 1)
                    if (s, n) == (1, 1) and last.exists:
                        wait(pe, att_done[0], last.times(1, 1))
                        if nxt.exists:
                            wait(pe, k_done[0], nxt.times(1, 1))
                        elif m.exists:
                            wait(pe, gate_done, m.times(HG, HG))
                        else:
                            wait(pe, y_done[0], last.times(CB, 0))
                        project(work[:, 1], wf0_sb, 0, att).then_inc(y_ps[0], 1)
                    if (s, n) == (2, 0) and far.exists:
                        wait(pe, g_done[0], far.times(1, 1))
                        wait(pe, v_done[0], nxt.times(1, 1))
                        for tb in range(TB):
                            for cb in range(CB):
                                ins = pe.transpose(work[:, 0, tb, cb * P:(cb + 1) * P],
                                                   g_sb[:, far.base % 2, cb, tb * P:(tb + 1) * P], ident[:])
                        ins.then_inc(t1_done, 1)
                    if (s, n) == (2, 1) and nxt.exists:
                        if last.exists:
                            wait(pe, y_done[0], last.times(CB, CB))
                        else:
                            wait(pe, k_done[0], nxt.times(1, 1))
                        project(work[:, 1], w0_sb, 3 * CH, src).then_inc(gate_ps, 1)
                    if (s, n) == (3, 0) and far.exists:
                        wait(pe, xn_done, far.times(TB, TB))
                        for cb in range(CB):
                            for tb in range(TB):
                                ins = pe.transpose(work[:, 0, cb, tb * P:(tb + 1) * P], xn[:, tb, cb * P:(cb + 1) * P],
                                                   ident[:])
                        ins.then_inc(t2_done, 1)

                for s in range(STEPS0):
                    r, g = (m, s + 2) if s < 2 else (nxt, s - 2)
                    if r.exists:
                        scores(r, g)
                    for n in range(2):
                        if m.exists:
                            turns(s, n)
                        task(s, n)
                    if m.exists:
                        mixes(s)

            over_rows(pe, 2, 1, body0)

            group_sums(1)
            pe.wait_ge(y_done[0], CB * ROWS)
            pe.wait_ge(prob1_clear, 1)

            def body1(m):
                last, nxt, far = m + -1, m + 1, m + 2
                src = g_sb[:, far.base % 2]

                def scores(r, g):
                    wait(pe, q_done[1], r.times(HP, HP))
                    wait(pe, k_done[1], r.times(HP, HP))
                    wait(pe, min_done[1], r.times(4 * HP, 4 * (g + 1 - HP)))
                    for ib in range(TB):
                        for a in range(2):
                            q = slice(a * D1, (a + 1) * D1)
                            j0 = ib * (TOK - WIN)
                            ins = pe.matmul(score[:, 2 * g + a, ib, 0:WIN], nqT[q, r.base % 2, g, ib * P:(ib + 1) * P],
                                            kT[q, r.base % 2, g, j0:j0 + WIN], start=True, stop=True)
                            if ib == TB - 1:
                                ins.then_inc(score_done[1], 1)

                def turns(g, a):
                    wait(pe, norm_done[1], m.times(4 * HP, 4 * g + 2 * (a + 1)))
                    if a == 0:
                        wait(pe, turn_done[1][1], m.times(HP, g))
                    else:
                        wait(pe, turn_done[1][0], m.times(HP, g + 1))
                    apart(pe, pe_passed)
                    p = prob1[:, m.base % 2, g, a]
                    pe.transpose(turn[:, P:WIN], p[0:HALO, 1, 0:P], ident[0:HALO, 0:HALO]).then_inc(halo_ps, 1)
                    pe.transpose(turn[:, 0:P], p[:, 0, 0:P], ident[:])
                    pe.transpose(turn[:, WIN + HALO:2 * WIN], p[:, 1, P:TOK], ident[:])
                    wait(pe, halo_ps, m.times(2 * HP, 2 * g + a + 1))
                    apart(pe, pe_passed)
                    pe.transpose(turn[:, WIN:WIN + HALO], p[P - HALO:P, 0, P:TOK], ident[P - HALO:P, P - HALO:P]
                                 ).then_inc(turn_ps[1][a], 1)

                def mixes(g):
                    wait(pe, v_done[1], m.times(1, 1))
                    wait(pe, att_done[1], m.times(1, 0))
                    for a in range(2):
                        wait(pe, turn_done[1][a], m.times(HP, g + 1))
                    for jb in range(TB):
                        i0 = jb * (TOK - WIN)
                        for a in range(2):
                            c = (2 * g + a) * D1
                            ins = pe.matmul(mix[a * D1:(a + 1) * D1, g, i0:i0 + WIN], v_sb[:, m.base % 4, jb, c:c + D1],
                                            probT1[:, g, a, jb * WIN:(jb + 1) * WIN], start=jb == 0, stop=jb == TB - 1,
                                            skip_group_check=True)
                    ins.then_inc(mix_ps[1], 1)

                for s in range(HP):
                    if nxt.exists:
                        scores(nxt, s)
                    if m.exists:
                        turns(s, 0)
                    if s == 0 and far.exists:
                        wait(pe, g_done[1], far.times(1, 1))
                        wait(pe, v_done[1], nxt.times(1, 1))
                        project(work[:, 0], w1_sb, 0, src).then_inc(q_ps[1], 1)
                    if m.exists:
                        turns(s, 1)
                    if s == 0 and last.exists:
                        wait(pe, att_done[1], last.times(1, 1))
                        if nxt.exists:
                            wait(pe, k_done[1], nxt.times(HP, HP))
                        else:
                            wait(pe, y_done[1], last.times(CB, 0))
                        project(work[:, 1], wf1_sb, 0, att).then_inc(y_ps[1], 1)
                    if s == 0 and far.exists:
                        if last.exists:
                            wait(pe, y_done[1], last.times(CB, CB))
                        else:
                            wait(pe, k_done[1], nxt.times(HP, HP))
                        project(work[:, 1], w1_sb, CH, src).then_inc(k_ps[1], 1)
                    if s == 1 and far.exists:
                        wait(pe, q_done[1], far.times(HP, HP))
                        project_tokens(work[:, 0], w1_sb, 2 * CH, src).then_inc(v_ps[1], 1)
                    if m.exists:
                        mixes(s)

            over_rows(pe, 2, 1, body1)

        @block.scalar
        def _(act):
            act.wait_ge(consts_in, 16 * 11)
            act.wait_ge(consts_set, 2)
            def pair_bias(plus):
                for b in range(2):
                    for ib in range(TB):
                        wait(act, bias_ps, plus(4, 2 * b + ib + 1))
                        apart(act, act_passed)
                        keys = bass.ds(plus(2 * JCHUNK, b * JCHUNK), JCHUNK)
                        act.activation(neg_bias[:, ib, :, keys].rearrange("p h j -> p j h"),
                                       score[:, 2 * b + ib, 0, 0:JCHUNK * H0].rearrange("p (j h) -> p j h", h=H0),
                                       ACT.Copy, scale=-float(D0) ** -0.5).then_inc(bias_done, 1)

            over_chunks(act, NJC, pair_bias)

            def body0(m):
                nxt, far = m + 1, m + 2

                def exps(r, g, a):
                    for ib in range(TB):
                        wait(act, min_done[0], r.times(4 * STEPS0, 4 * g + 2 * a + ib + 1))
                        act.activation(prob[:, g, a, ib], prob[:, g, a, ib], ACT.Exp, bias=row_min[:, g, a, ib:ib + 1],
                                       scale=-1.0, accum_out=row_sum[:, g, a, ib:ib + 1]).then_inc(exp_done[0], 1)

                for s in range(STEPS0):
                    r, g = (m, s + 2) if s < 2 else (nxt, s - 2)
                    if m.exists:
                        wait(act, turn_ps[0][0], m.times(STEPS0, s + 1))
                        wait(act, mix_ps[0], m.times(STEPS0, s - 1))
                        act.copy(probT[:, s % 2, 0], turn[:]).then_inc(turn_done[0][0], 1)
                    if r.exists:
                        exps(r, g, 0)
                    if s == 0 and nxt.exists:
                        wait(act, k_ps[0], nxt.times(1, 1))
                        act.copy(kT[:, nxt.base % 2], work[:, 1]).then_inc(k_done[0], 1)
                    if s == 1 and nxt.exists:
                        wait(act, v_ps[0], nxt.times(1, 1))
                        act.copy(v_sb[:, nxt.base % 2], work[:, 0]).then_inc(v_done[0], 1)
                    if r.exists:
                        exps(r, g, 1)
                    if s == 2 and nxt.exists:
                        wait(act, gate_ps, nxt.times(1, 1))
                        wait(act, att_done[0], nxt.times(1, -1))
                        for hg in range(HG):
                            act.activation(gate[:, nxt.base % 2, hg], work[:, 1, hg], ACT.Tanh, scale=0.5,
                                           bias=half_gate_b[:, hg:hg + 1]).then_inc(gate_done, 1)
                    if s == 3 and far.exists:
                        wait(act, t2_done, far.times(1, 1))
                        for cb in range(CB):
                            act.activation(xnT[:, far.base % 2, cb], work[:, 0, cb], ACT.Identity,
                                           scale=vec0_sb[:, 0, cb:cb + 1], bias=vec0_sb[:, 1, cb:cb + 1]
                                           ).then_inc(xnT_done, 1)

            over_rows(act, 2, 0, body0)

            def body1(m):
                last, nxt, far = m + -1, m + 1, m + 2
                for s in range(HP):
                    if s == 0 and last.exists:
                        wait(act, mix_ps[1], last.times(HP, HP))
                        wait(act, y_ps[1], last.times(1, 0))
                        act.copy(att[:], mix[:]).then_inc(att_done[1], 1)
                    if m.exists:
                        wait(act, turn_ps[1][0], m.times(HP, s + 1))
                        wait(act, mix_ps[1], m.times(HP, s + 1 - HP))
                        act.copy(probT1[:, s, 0], turn[:, 0:2 * WIN]).then_inc(turn_done[1][0], 1)
                    for a in range(2):
                        if nxt.exists:
                            for ib in range(TB):
                                w = prob1[:, nxt.base % 2, s, a, ib, ib * (TOK - WIN):ib * (TOK - WIN) + WIN]
                                wait(act, min_done[1], nxt.times(4 * HP, 4 * s + 2 * a + ib + 1))
                                act.activation(w, w, ACT.Exp, bias=row_min1[:, nxt.base % 2, s, a, ib:ib + 1], scale=-1.0,
                                               accum_out=row_sum1[:, nxt.base % 2, s, a, ib:ib + 1]).then_inc(exp_done[1], 1)
                    if s == 0 and far.exists:
                        wait(act, k_ps[1], far.times(1, 1))
                        for hp in range(HP):
                            act.activation(kT[:, far.base % 2, hp], work[:, 1, hp], ACT.Identity,
                                           bias=vec1_sb[:, 1, hp:hp + 1]).then_inc(k_done[1], 1)

            over_rows(act, 2, 1, body1)

        @block.vector
        def _(dve):
            dve.wait_ge(consts_in, 16 * 11)
            dve.tensor_scalar(half_gate_b[:], vec0_sb[:, 2], 0.5, None, ALU.mult).then_inc(consts_set, 1)
            dve.tensor_scalar(wf0_sb[:], wf0_sb[:], 0.5, None, ALU.mult).then_inc(wf0_halved, 1)
            dve.wait_ge(consts_set, 2)

            def x_stats(plus):
                for b in range(2):
                    wait(dve, x_chunk_in[b], plus(16, 16))
                    apart(dve, dve_passed)
                    for cb in range(CB):
                        for t in range(XCHUNK // 512):
                            at = bass.ds(plus(2 * XCHUNK // 512, b * (XCHUNK // 512) + t), 1)
                            dve.bn_stats(gstat0[:, cb, at], x_chunk[:, b, cb, t * 512:(t + 1) * 512]
                                         ).then_inc(x_chunk_used, 1)

            over_chunks(dve, NXC, x_stats)

            def group_norm(n, stat):
                for cb in range(CB):
                    dve.bn_aggr(ch_mv[:, cb], stat[:, cb].rearrange("p n s -> p (n s)")).then_inc(gn_chain[n], 1)
                dve.wait_ge(gn_ps[n], 1)
                dve.tensor_copy(gn_mean[:], mix[:, 0, 0:CB]).then_inc(gn_chain[n], 1)
                dve.wait_ge(gn_chain[n], 3)
                dve.tensor_tensor(gn_dev[:], ch_mv[:, :, 0], gn_mean[:], ALU.subtract).then_inc(gn_chain[n], 1)
                dve.wait_ge(gn_chain[n], 4)
                dve.tensor_tensor(gn_sq[:], gn_dev[:], gn_dev[:], ALU.mult).then_inc(gn_chain[n], 1)
                dve.wait_ge(gn_chain[n], 5)
                dve.tensor_tensor(gn_sq[:], gn_sq[:], ch_mv[:, :, 1], ALU.add).then_inc(gn_chain[n], 1)
                dve.wait_ge(gn_ps[n], 2)
                dve.tensor_scalar(gn_var[:], mix[:, 0, CB:2 * CB], EPS, None, ALU.add).then_inc(gn_chain[n], 1)
                dve.wait_ge(gn_rstd[n], 1)
                dve.scalar_tensor_tensor(out=gn_shift[n][:], in0=gn_mean[:], scalar=-1.0, in1=gn_scale[n][:],
                                         op0=ALU.mult, op1=ALU.mult).then_inc(gn_ready[n], 1)

            dve.wait_ge(x_chunk_used, 8 * NXC)
            group_norm(0, gstat0)
            dve.wait_ge(bias_done, TB * NJC)

            def residual(n, last, bias):
                wait(dve, y_ps[n], last.times(1, 1))
                wait(dve, y_out[n][last.base % 2], last.times(16, 0, of=2))
                for ob in range(CB):
                    dve.scalar_tensor_tensor(out=y_sb[:, last.base % 2, ob], in0=work[:, 1, ob], scalar=bias[:, ob:ob + 1],
                                             in1=x_sb[:, last.base % XSLOTS, ob], op0=ALU.add, op1=ALU.add
                                             ).then_inc(y_done[n], 1)

            def body0(m):
                last, nxt, far = m + -1, m + 1, m + 2

                def mins(r, g, a):
                    wait(dve, score_done[0], r.times(2 * STEPS0, 2 * g + a + 1))
                    wait(dve, turn_ps[0][a], r.times(STEPS0, g + 1 - STEPS0))
                    apart(dve, dve_passed)
                    for ib in range(TB):
                        dve.tensor_tensor_reduce(prob[:, g, a, ib], score[:, (2 * g + a) % HPG, ib],
                                                 neg_bias[:, ib, 2 * g + a], 1.0, 3.0e38, ALU.add, ALU.min,
                                                 row_min[:, g, a, ib:ib + 1]).then_inc(min_done[0], 1)

                for s in range(STEPS0):
                    r, g = (m, s + 1) if s + 1 < STEPS0 else (nxt, 0)
                    if r.exists:
                        wait(dve, exp_done[0], r.times(4 * STEPS0, 4 * (g + 1)))
                        dve.reciprocal(row_inv[:, g], row_sum[:, g]).then_inc(inv_done[0], 1)
                    if s == 0 and last.exists:
                        wait(dve, mix_ps[0], last.times(STEPS0, STEPS0))
                        wait(dve, gate_done, last.times(HG, HG))
                        wait(dve, y_ps[0], last.times(1, 0))
                        dve.scalar_tensor_tensor(out=att[:], in0=gate[:, last.base % 2], scalar=1.0, in1=mix[:],
                                                 op0=ALU.add, op1=ALU.mult).then_inc(att_done[0], 1)
                    r, g = (m, s + 2) if s < 2 else (nxt, s - 2)
                    if r.exists:
                        mins(r, g, 0)
                    if s == 0 and nxt.exists:
                        wait(dve, q_ps[0], nxt.times(1, 1))
                        dve.tensor_scalar(nqT[:, nxt.base % 2], work[:, 0], -1.0, None, ALU.mult).then_inc(q_done[0], 1)
                    if s == 2 and far.exists:
                        wait(dve, t1_done, far.times(1, 1))
                        for tb in range(TB):
                            dve.bn_stats(ln_st[:, tb], work[:, 0, tb]).then_inc(ln_chain, 1)
                        for tb in range(TB):
                            wait(dve, ln_chain, far.times(2 * TB, tb + 1))
                            apart(dve, dve_passed)
                            dve.bn_aggr(ln_mv[:, tb], ln_st[:, tb]).then_inc(ln_chain, 1)
                        wait(dve, ln_chain, far.times(2 * TB, 2 * TB))
                        dve.tensor_scalar(ln_var[:], ln_mv[:, :, 1], EPS, None, ALU.add).then_inc(ln_var_done, 1)
                    if m.exists:
                        wait(dve, turn_ps[0][1], m.times(STEPS0, s + 1))
                        wait(dve, mix_ps[0], m.times(STEPS0, s - 1))
                        dve.tensor_copy(probT[:, s % 2, 1], turn[:]).then_inc(turn_done[0][1], 1)
                    if r.exists:
                        mins(r, g, 1)
                    if s == 1 and last.exists:
                        residual(0, last, vec0_sb[:, 3])
                        for ob in range(CB):
                            wait(dve, y_done[0], last.times(CB, ob + 1))
                            apart(dve, dve_passed)
                            at = slice(last.base, last.base + 1) if last.loop is None else bass.ds(last.times(1), 1)
                            dve.bn_stats(gstat1[:, ob, at], y_sb[:, last.base % 2, ob]).then_inc(y_stats, 1)
                    if s == 2 and far.exists:
                        wait(dve, ln_rstd_done, far.times(1, 1))
                        wait(dve, t2_done, far.times(1, 0))
                        for tb in range(TB):
                            dve.tensor_scalar(xn[:, tb], work[:, 0, tb], ln_mv[:, tb, 0:1], ln_rstd[:, tb:tb + 1],
                                              ALU.subtract, ALU.mult).then_inc(xn_done, 1)

            over_rows(dve, 2, 1, body0)

            dve.wait_ge(y_stats, CB * ROWS)
            group_norm(1, gstat1)
            dve.wait_ge(prob1_clear, 1)

            def body1(m):
                last, nxt, far = m + -1, m + 1, m + 2
                for s in range(HP):
                    r, g = (m, 1) if s == 0 else (nxt, 0)
                    if r.exists:
                        wait(dve, exp_done[1], r.times(4 * HP, 4 * (g + 1)))
                        dve.reciprocal(row_inv1[:, r.base % 2, g], row_sum1[:, r.base % 2, g]).then_inc(inv_done[1], 1)
                    for a in range(2):
                        if nxt.exists:
                            wait(dve, score_done[1], nxt.times(2 * HP, 2 * s + a + 1))
                            wait(dve, turn_ps[1][a], nxt.times(HP, s + 1 - 2 * HP))
                            apart(dve, dve_passed)
                            for ib in range(TB):
                                j0 = ib * (TOK - WIN)
                                dve.tensor_tensor_reduce(prob1[:, nxt.base % 2, s, a, ib, j0:j0 + WIN],
                                                         score[:, 2 * s + a, ib, 0:WIN], band[:, ib],
                                                         1.0, 3.0e38, ALU.add, ALU.min,
                                                         row_min1[:, nxt.base % 2, s, a, ib:ib + 1]).then_inc(min_done[1], 1)
                        if a == 0 and m.exists:
                            wait(dve, turn_ps[1][1], m.times(HP, s + 1))
                            wait(dve, mix_ps[1], m.times(HP, s + 1 - HP))
                            dve.tensor_copy(probT1[:, s, 1], turn[:, 0:2 * WIN]).then_inc(turn_done[1][1], 1)
                        if s == 0 and a == 0 and far.exists:
                            wait(dve, q_ps[1], far.times(1, 1))
                            for hp in range(HP):
                                dve.tensor_scalar(nqT[:, far.base % 2, hp], work[:, 0, hp], vec1_sb[:, 0, hp:hp + 1],
                                                  -float(D1) ** -0.5, ALU.add, ALU.mult).then_inc(q_done[1], 1)
                        if s == 0 and a == 0 and last.exists:
                            residual(1, last, vec1_sb[:, 2])
                    if s == 1 and far.exists:
                        wait(dve, v_ps[1], far.times(1, 1))
                        dve.tensor_tensor(v_sb[:, far.base % 4], work[:, 0], bv1_sb[:].unsqueeze(1).broadcast_to([P, TB, CH]),
                                          ALU.add).then_inc(v_done[1], 1)

            over_rows(dve, 2, 1, body1)


def channels(v):
    return np.asarray(v).reshape(CB, P).T


def rows_first(w, cols):
    return np.ascontiguousarray(np.asarray(w).reshape(CB, P, cols).transpose(1, 0, 2))


def kernel(**inputs):
    import concourse.bacc as bacc
    from concourse.bass_utils import run_bass_kernel_spmd

    a = {k: np.asarray(v) for k, v in inputs.items()}
    xT = np.ascontiguousarray(a["x"][0].transpose(2, 0, 1)).reshape(CH, ROWS * TOK)
    pairT = np.ascontiguousarray(a["L0_conv_x2d"][0].transpose(2, 1, 0))
    qkv = a["L0_conv_qkv_w"].reshape(D0, 3, H0, CH).transpose(3, 1, 2, 0).reshape(CH, 3 * CH)
    gate = a["L0_conv_gate_w"].reshape(D0, H0, CH).transpose(2, 1, 0).reshape(CH, CH)
    gate_b = a["L0_conv_gate_b"].reshape(D0, H0).T.reshape(CH)
    final = a["L0_conv_final_w"].T.reshape(D0, H0, CH).transpose(1, 0, 2).reshape(CH, CH)
    b_in = a["L1_conv_b_in"]

    c = np.arange(P)
    group_mean = np.where(c[:, None] // GROUP == c[None, :] // GROUP, 1.0 / GROUP, 0.0).astype(np.float32)
    queries = c[:, None, None] + P * np.arange(TB)[None, :, None]
    keys = np.arange(WIN)[None, None, :] + (TOK - WIN) * np.arange(TB)[None, :, None]
    band = np.where(abs(queries - keys) <= BAND, 0.0, FAR).astype(np.float32)

    arrays = {
        "xT": xT,
        "pairT": pairT,
        "w0": rows_first(np.concatenate([qkv, gate], axis=1), 4 * CH),
        "wf0": rows_first(final, CH),
        "pair_w": np.ascontiguousarray(a["L0_conv_x2d_w"].T),
        "vec0": np.ascontiguousarray(np.stack([channels(v) for v in (
            a["L0_conv_norm_w"], a["L0_conv_norm_b"], gate_b, a["L0_conv_final_b"])], axis=1)),
        "w1": rows_first(a["L1_conv_w_in"].T, 3 * CH),
        "wf1": rows_first(a["L1_conv_w_out"].T, CH),
        "vec1": np.ascontiguousarray(np.stack([channels(v) for v in (
            b_in[:CH], b_in[CH:2 * CH], a["L1_conv_b_out"])], axis=1)),
        "bv1": np.ascontiguousarray(b_in[2 * CH:].reshape(1, CH)),
        "ident_d": np.eye(P, dtype=np.float32),
        "group_d": group_mean,
        "band_d": band,
    }
    nc = bacc.Bacc("TRN2", target_bir_lowering=False, num_devices=1)
    aps = {n: nc.dram_tensor(n, v.shape, F32, kind="ExternalInput").ap() for n, v in arrays.items()}
    aps["x1T"] = nc.dram_tensor("x1T", (CH, ROWS * TOK), F32, kind="Internal").ap()
    aps["outT"] = nc.dram_tensor("outT", (CH, ROWS * TOK), F32, kind="ExternalOutput").ap()
    conv_preact_kernel(nc, **aps)
    r = run_bass_kernel_spmd(nc, [arrays], core_ids=[0])
    out = r.results[0]["outT"].reshape(CH, ROWS, TOK).transpose(1, 2, 0)
    return np.ascontiguousarray(out).reshape(1, ROWS, TOK, CH)
```

```python
from contextlib import ExitStack

import numpy as np

import concourse.bass as bass
from concourse import mybir

F32 = mybir.dt.float32
F32R = mybir.dt.float32r
ALU = mybir.AluOpType
ACT = mybir.ActivationFunctionType

P = 128
ROWS, TOK, CH = 128, 256, 256
CB = CH // P
TB = TOK // P
GROUP = CH // 32
EPS = 1e-5

H0, D0 = 8, 32
HG = H0 * D0 // P
HPG = P // D0
STEPS0 = H0 // 2
PAIR = 128

H1, D1 = 4, 64
HP = H1 // 2
BAND = 16
HALO = 32
WIN = P + HALO
FAR = 1.0e30

HIGH, LOW = 0, 1
PRODUCTS = ((HIGH, HIGH), (LOW, HIGH), (HIGH, LOW))

UNROLL = 4
XSLOTS = 4

XCHUNK = 1024
JCHUNK = 8


class Row:

    def __init__(self, loop, base):
        self.loop, self.base = loop, base

    def __add__(self, n):
        return Row(self.loop, self.base + n)

    @property
    def exists(self):
        return self.loop is not None or 0 <= self.base < ROWS

    def times(self, per, plus=0, of=1):
        fixed = per * (self.base // of) + plus
        return fixed if self.loop is None else self.loop * (per * UNROLL // of) + fixed

    def tokens(self):
        return bass.ds(self.times(TOK), TOK)


def wait(eng, sem, value):
    if isinstance(value, int):
        if value > 0:
            eng.wait_ge(sem, value)
    else:
        eng.wait_ge(sem, value)


def over_rows(eng, before, after, body):
    for m in range(-before, UNROLL):
        body(Row(None, m))
    with eng.Fori(0, ROWS // UNROLL - 2) as i:
        for k in range(UNROLL):
            body(Row(i, UNROLL + k))
    for m in range(ROWS - UNROLL, ROWS + after):
        body(Row(None, m))


def over_chunks(eng, count, body):
    body(lambda per, fixed: fixed)
    with eng.Fori(0, count // 2 - 1) as i:
        body(lambda per, fixed: i * per + (per + fixed))


def conv_preact_kernel(nc, xT, pairT, w0_d, wf0_d, pair_w, vec0, w1_d, wf1_d, vec1, bv1, ident_d, group_d, band_d, x1T, outT):
    x_v = xT.rearrange("(c p) t -> p c t", p=P)
    x1_v = x1T.rearrange("(c p) t -> p c t", p=P)
    out_v = outT.rearrange("(c p) t -> p c t", p=P)

    with ExitStack() as ctx:
        def sb(name, shape, dt=F32):
            return ctx.enter_context(nc.sbuf_tensor(name, shape, dt))

        def sem(name):
            return ctx.enter_context(nc.semaphore(name))

        ident = sb("ident", [P, P])
        group_mean = sb("group_mean", [P, P])
        band = sb("band", [P, TB, WIN])
        w0 = sb("w0", [P, 2, CB, 4 * CH], F32R)
        wf0 = sb("wf0", [P, 2, CB, CH], F32R)
        pairw_sb = sb("pairw_sb", [P, H0])
        vec0_sb = sb("vec0_sb", [P, 4, CB])
        w1 = sb("w1", [P, 2, CB, 3 * CH], F32R)
        wf1 = sb("wf1", [P, 2, CB, CH], F32R)
        vec1_sb = sb("vec1_sb", [P, 3, CB])
        bv1_sb = sb("bv1_sb", [P, CH])
        minus_half = sb("minus_half", [P, CB])
        half_gate_b = sb("half_gate_b", [P, CB])
        b_q1 = sb("b_q1", [P, CB])
        gstat0 = sb("gstat0", [P, CB, ROWS * TOK // 512, 6])
        gstat1 = sb("gstat1", [P, CB, ROWS, 6])
        ch_mv = sb("ch_mv", [P, CB, 2])
        gn_mean = sb("gn_mean", [P, CB])
        gn_dev = sb("gn_dev", [P, CB])
        gn_sq = sb("gn_sq", [P, CB])
        gn_var = sb("gn_var", [P, CB])
        gn_scale = [sb(f"gn_scale{n}", [P, CB]) for n in range(2)]
        gn_shift = [sb(f"gn_shift{n}", [P, CB]) for n in range(2)]
        x_chunk = sb("x_chunk", [P, 2, CB, XCHUNK])
        pair_chunk = sb("pair_chunk", [P, 2, JCHUNK, TOK])
        neg_bias = sb("neg_bias", [P, TB, H0, TOK])
        x_sb = sb("x_sb", [P, XSLOTS, CB, TOK])
        g_sb = sb("g_sb", [P, 2, CB, TOK])
        ln_st = sb("ln_st", [P, TB, 6])
        ln_mv = sb("ln_mv", [P, TB, 2])
        ln_var = sb("ln_var", [P, TB])
        ln_rstd = sb("ln_rstd", [P, TB])
        xn = sb("xn", [P, TB, CH])
        xnT = sb("xnT", [P, CB, TOK])
        src = sb("src", [P, 2, 2, CB, TOK], F32R)
        nqT = sb("nqT", [P, 2, 2, CB, TOK], F32R)
        kT = sb("kT", [P, 2, 2, CB, TOK], F32R)
        v_sb = sb("v_sb", [P, 4, TB, CH])
        gate = sb("gate", [P, 2, HG, TOK])
        prob = sb("prob", [P, STEPS0, 2, TB, TOK])
        row_min = sb("row_min", [P, STEPS0, 2, TB])
        row_sum = sb("row_sum", [P, STEPS0, 2, TB])
        row_inv = sb("row_inv", [P, STEPS0, 2, TB])
        probT = sb("probT", [P, 2, 2, TB, TOK])
        att_sum = sb("att_sum", [P, HG, TOK])
        att = sb("att", [P, 2, HG, TOK], F32R)
        y_sb = sb("y_sb", [P, 2, CB, TOK])
        prob1 = prob[:].rearrange("p (r g) a b t -> p r g a b t", r=2)
        row_min1 = sb("row_min1", [P, 2, HP, 2, TB])
        row_sum1 = sb("row_sum1", [P, 2, HP, 2, TB])
        row_inv1 = sb("row_inv1", [P, 2, HP, 2, TB])
        probT1 = probT[:].rearrange("p s a b t -> p s a (b t)")[:, :, :, 0:2 * WIN]
        stage = prob[:].rearrange("p g a b t -> p (g a b t)")
        sizes = (4 * CH, CH, 3 * CH)
        starts = (0, CB * 4 * CH, CB * 5 * CH)
        w0_in, wf0_in, w1_in = (stage[:, s0:s0 + CB * n].rearrange("p (c n) -> p c n", c=CB)
                                for s0, n in zip(starts, sizes))
        wf1_in = probT[:].rearrange("p s a b t -> p (s a b t)")[:, 0:CB * CH].rearrange("p (c n) -> p c n", c=CB)

        score = ctx.enter_context(nc.psum_tensor("score", [P, 4, TB, TOK], F32))
        turn = ctx.enter_context(nc.psum_tensor("turn", [P, 2 * TOK], F32))
        mix = ctx.enter_context(nc.psum_tensor("mix", [P, 2, TOK], F32))
        work = ctx.enter_context(nc.psum_tensor("work", [P, 2, 2, TOK], F32))

        consts_in = sem("consts_in")
        consts_set = sem("consts_set")
        high_set = sem("high_set")
        weights_set = sem("weights_set")
        x_chunk_in = [sem(f"x_chunk_in{n}") for n in range(2)]
        x_chunk_used = sem("x_chunk_used")
        pair_in = [sem(f"pair_in{n}") for n in range(2)]
        bias_ps = sem("bias_ps")
        bias_done = sem("bias_done")
        gn_chain = [sem(f"gn_chain{n}") for n in range(2)]
        gn_ps = [sem(f"gn_ps{n}") for n in range(2)]
        gn_rstd = [sem(f"gn_rstd{n}") for n in range(2)]
        gn_ready = [sem(f"gn_ready{n}") for n in range(2)]

        x_in = [[sem(f"x_in{n}_{s}") for s in range(XSLOTS)] for n in range(2)]
        g_done = [sem(f"g_done{n}") for n in range(2)]
        t1_done = sem("t1_done")
        ln_chain = sem("ln_chain")
        ln_var_done = sem("ln_var_done")
        ln_rstd_done = sem("ln_rstd_done")
        xn_done = sem("xn_done")
        t2_done = sem("t2_done")
        xnT_done = sem("xnT_done")
        q_ps = [sem(f"q_ps{n}") for n in range(2)]
        k_ps = [sem(f"k_ps{n}") for n in range(2)]
        v_ps = [sem(f"v_ps{n}") for n in range(2)]
        gate_ps = sem("gate_ps")
        y_ps = [sem(f"y_ps{n}") for n in range(2)]
        src_high = [sem(f"src_high{n}") for n in range(2)]
        src_done = [sem(f"src_done{n}") for n in range(2)]
        q_high = [sem(f"q_high{n}") for n in range(2)]
        k_high = [sem(f"k_high{n}") for n in range(2)]
        att_sum_done = sem("att_sum_done")
        att_high = [sem(f"att_high{n}") for n in range(2)]
        q_done = [sem(f"q_done{n}") for n in range(2)]
        k_done = [sem(f"k_done{n}") for n in range(2)]
        v_done = [sem(f"v_done{n}") for n in range(2)]
        gate_done = sem("gate_done")
        y_done = [sem(f"y_done{n}") for n in range(2)]
        y_stats = sem("y_stats")
        score_done = [sem(f"score_done{n}") for n in range(2)]
        min_done = [sem(f"min_done{n}") for n in range(2)]
        exp_done = [sem(f"exp_done{n}") for n in range(2)]
        inv_done = [sem(f"inv_done{n}") for n in range(2)]
        norm_done = [sem(f"norm_done{n}") for n in range(2)]
        turn_ps = [[sem(f"turn_ps{n}_{a}") for a in range(2)] for n in range(2)]
        turn_done = [[sem(f"turn_done{n}_{a}") for a in range(2)] for n in range(2)]
        halo_ps = sem("halo_ps")
        mix_ps = [sem(f"mix_ps{n}") for n in range(2)]
        att_done = [sem(f"att_done{n}") for n in range(2)]
        prob1_clear = sem("prob1_clear")
        y_out = [[sem(f"y_out{n}_{s}") for s in range(2)] for n in range(2)]

        NXC = ROWS * TOK // XCHUNK
        XSTATS = CB * XCHUNK // 512
        NJC = TOK // JCHUNK

        pool_passed, act_passed, dve_passed, sp_passed, pe_passed = (
            sem(f"{e}_passed") for e in ("pool", "act", "dve", "sp", "pe"))

        def apart(eng, passed):
            eng.sem_inc(passed, 1)

        everything = slice(0, CH)
        weights = ((w0, w0_in, ((everything, -1.0), (slice(CH, 4 * CH), 1.0))),
                   (wf0, wf0_in, ((everything, 0.5),)),
                   (w1, w1_in, ((everything, -float(D1) ** -0.5), (slice(CH, 3 * CH), 1.0))),
                   (wf1, wf1_in, ((everything, 1.0),)))

        def bank0(m, use):
            return (m.base + use) % 2

        block = ctx.enter_context(nc.Block())

        @block.sync
        def _(sp):
            for to, of in ((w0_in, w0_d), (wf0_in, wf0_d), (w1_in, w1_d), (wf1_in, wf1_d), (ident[:], ident_d),
                           (group_mean[:], group_d), (band[:], band_d), (pairw_sb[:], pair_w), (vec0_sb[:], vec0),
                           (vec1_sb[:], vec1)):
                sp.dma_start(to, of).then_inc(consts_in, 16)
            sp.dma_start(bv1_sb[:], bv1.broadcast_to([P, CH])).then_inc(consts_in, 16)

            def chunks(plus):
                for b in range(2):
                    wait(sp, x_chunk_used, plus(2 * XSTATS, XSTATS * (b - 1)))
                    apart(sp, sp_passed)
                    sp.dma_start(x_chunk[:, b], x_v[:, :, bass.ds(plus(2 * XCHUNK, b * XCHUNK), XCHUNK)]
                                 ).then_inc(x_chunk_in[b], 16)
                    wait(sp, bias_ps, plus(4, 2 * b - 2))
                    apart(sp, sp_passed)
                    sp.dma_start(pair_chunk[:, b], pairT[:, bass.ds(plus(2 * JCHUNK, b * JCHUNK), JCHUNK), :]
                                 ).then_inc(pair_in[b], 16)

            over_chunks(sp, NXC, chunks)

            def rows(n, of, to):
                def body(m):
                    if (m + -1).exists:
                        wait(sp, y_done[n], m.times(CB))
                        apart(sp, sp_passed)
                        sp.dma_start(to[:, :, (m + -1).tokens()], y_sb[:, (m.base - 1) % 2]
                                     ).then_inc(y_out[n][(m.base - 1) % 2], 16)
                    if (m + 3).exists and (m.loop is not None or m.base + 3 < ROWS):
                        slot = (m.base + 3) % XSLOTS
                        sp.dma_start(x_sb[:, slot], of[:, :, (m + 3).tokens()]).then_inc(x_in[n][slot], 16)

                over_rows(sp, 3, 1, body)
                for s in range(2):
                    sp.wait_ge(y_out[n][s], 16 * ROWS // 2)

            rows(0, x_v, x1_v)
            rows(1, x1_v, out_v)

        @block.gpsimd
        def _(pool):
            pool.memset(minus_half[:], -0.5).then_inc(consts_set, 1)

            def power(n):
                pool.wait_ge(consts_set, 2)
                pool.wait_ge(gn_chain[n], 7)
                pool.tensor_tensor(gn_scale[n][:], gn_var[:], minus_half[:], ALU.pow).then_inc(gn_rstd[n], 1)
                pool.wait_ge(gn_ready[n], 1)

            def affine(n, m, waits):
                wait(pool, x_in[n][m.base % XSLOTS], m.times(16, 16, of=XSLOTS))
                waits()
                apart(pool, pool_passed)
                for cb in range(CB):
                    ins = pool.tensor_scalar(g_sb[:, m.base % 2, cb], x_sb[:, m.base % XSLOTS, cb],
                                             gn_scale[n][:, cb:cb + 1], gn_shift[n][:, cb:cb + 1], ALU.mult, ALU.add)
                ins.then_inc(g_done[n], 1)

            power(0)

            def body0(m):
                for s in range(STEPS0):
                    r, g = (m, s + 1) if s + 1 < STEPS0 else (m + 1, 0)
                    if r.exists:
                        wait(pool, inv_done[0], r.times(STEPS0, g + 1))
                        apart(pool, pool_passed)
                        for a in range(2):
                            for ib in range(TB):
                                pool.tensor_scalar(prob[:, g, a, ib], prob[:, g, a, ib], row_inv[:, g, a, ib:ib + 1],
                                                   1.0, ALU.mult, ALU.mult).then_inc(norm_done[0], 1)
                    if s == 0 and (m + 2).exists:
                        affine(0, m + 2, lambda: wait(pool, t1_done, (m + 2).times(1, -1)))
                    if s == 1 and (m + 2).exists:
                        wait(pool, ln_var_done, (m + 2).times(1, 1))
                        apart(pool, pool_passed)
                        pool.tensor_tensor(ln_rstd[:], ln_var[:], minus_half[:], ALU.pow).then_inc(ln_rstd_done, 1)

            over_rows(pool, 2, 0, body0)

            pool.wait_ge(turn_ps[0][1], STEPS0 * ROWS)
            pool.memset(prob[:], 0.0).then_inc(prob1_clear, 1)
            power(1)

            def body1(m):
                for s in range(HP):
                    if s == 0 and (m + 2).exists:
                        affine(1, m + 2, lambda: wait(pool, src_done[1], (m + 2).times(1, -1)))
                    r, g = (m, 1) if s == 0 else (m + 1, 0)
                    if r.exists:
                        wait(pool, inv_done[1], r.times(HP, g + 1))
                        apart(pool, pool_passed)
                        for a in range(2):
                            for ib in range(TB):
                                w = prob1[:, r.base % 2, g, a, ib, ib * (TOK - WIN):ib * (TOK - WIN) + WIN]
                                pool.tensor_scalar(w, w, row_inv1[:, r.base % 2, g, a, ib:ib + 1], 1.0,
                                                   ALU.mult, ALU.mult).then_inc(norm_done[1], 1)

            over_rows(pool, 2, 0, body1)

        @block.tensor
        def _(pe):
            pe.wait_ge(consts_in, 16 * 11)
            def pair_bias(plus):
                for b in range(2):
                    wait(pe, pair_in[b], plus(16, 16))
                    wait(pe, bias_done, plus(4, 2 * b - 2))
                    for ib in range(TB):
                        for j in range(JCHUNK):
                            ins = pe.matmul(score[:, 2 * b + ib, 0, j * H0:(j + 1) * H0],
                                            pair_chunk[:, b, j, ib * P:(ib + 1) * P], pairw_sb[:],
                                            start=True, stop=True)
                        ins.then_inc(bias_ps, 1)

            over_chunks(pe, NJC, pair_bias)

            def group_sums(n):
                pe.wait_ge(gn_chain[n], 2)
                pe.matmul(mix[:, 0, 0:CB], group_mean[:], ch_mv[:, :, 0], start=True, stop=True).then_inc(gn_ps[n], 1)
                pe.wait_ge(gn_chain[n], 6)
                pe.matmul(mix[:, 0, CB:2 * CB], group_mean[:], gn_sq[:], start=True, stop=True).then_inc(gn_ps[n], 1)

            group_sums(0)
            pe.wait_ge(weights_set, sum(len(scales) for _, _, scales in weights))

            def project(out, w, cols, x):
                for cb in range(CB):
                    terms = [(kb, part) for kb in range(CB) for part in PRODUCTS]
                    for n, (kb, (of_w, of_x)) in enumerate(terms):
                        ins = pe.matmul(out[:, cb], w[:, of_w, kb, cols + cb * P:cols + (cb + 1) * P], x[:, of_x, kb],
                                        start=n == 0, stop=n == len(terms) - 1)
                return ins

            def project_tokens(out, w, cols, x):
                for tb in range(TB):
                    terms = [(kb, part) for kb in range(CB) for part in PRODUCTS]
                    for n, (kb, (of_w, of_x)) in enumerate(terms):
                        ins = pe.matmul(out[:, tb], x[:, of_x, kb, tb * P:(tb + 1) * P], w[:, of_w, kb, cols:cols + CH],
                                        start=n == 0, stop=n == len(terms) - 1)
                return ins

            def body0(m):
                last, nxt, far = m + -1, m + 1, m + 2
                x = src[:, nxt.base % 2]

                def scores(r, g):
                    wait(pe, q_done[0], r.times(1, 1))
                    wait(pe, k_done[0], r.times(1, 1))
                    wait(pe, min_done[0], r.times(4 * STEPS0, 4 * (g - 1)))
                    for ib in range(TB):
                        for n, (of_q, of_k) in enumerate(PRODUCTS):
                            for a in range(2):
                                hg, h = divmod(2 * g + a, HPG)
                                q = slice(h * D0, (h + 1) * D0)
                                ins = pe.matmul(score[:, h, ib], nqT[q, r.base % 2, of_q, hg, ib * P:(ib + 1) * P],
                                                kT[q, r.base % 2, of_k, hg], start=n == 0, stop=n == len(PRODUCTS) - 1)
                                if ib == TB - 1 and n == len(PRODUCTS) - 1:
                                    ins.then_inc(score_done[0], 1)

                def turns(g, a):
                    wait(pe, norm_done[0], m.times(4 * STEPS0, 4 * g + 2 * (a + 1)))
                    if a == 0:
                        wait(pe, turn_done[0][1], m.times(STEPS0, g))
                    else:
                        wait(pe, turn_done[0][0], m.times(STEPS0, g + 1))
                    for jb in range(TB):
                        for ib in range(TB):
                            ins = pe.transpose(turn[:, jb * TOK + ib * P:jb * TOK + (ib + 1) * P],
                                               prob[:, g, a, ib, jb * P:(jb + 1) * P], ident[:])
                    ins.then_inc(turn_ps[0][a], 1)

                def mixes(r, g):
                    wait(pe, v_done[0], r.times(1, 1))
                    wait(pe, att_sum_done, r.times(1, 0))
                    for a in range(2):
                        wait(pe, turn_done[0][a], r.times(STEPS0, g + 1))
                    for jb in range(TB):
                        for a in range(2):
                            hg, h = divmod(2 * g + a, HPG)
                            c = (2 * g + a) * D0
                            ins = pe.matmul(mix[h * D0:(h + 1) * D0, hg], v_sb[:, r.base % 2, jb, c:c + D0],
                                            probT[:, g % 2, a, jb], start=jb == 0, stop=jb == TB - 1,
                                            skip_group_check=True)
                    ins.then_inc(mix_ps[0], 1)

                def task(s, n):
                    if (s, n) == (0, 0) and nxt.exists:
                        wait(pe, src_done[0], nxt.times(1, 1))
                        project(work[:, bank0(m, 0)], w0, 0, x).then_inc(q_ps[0], 1)
                    if (s, n) == (0, 1) and nxt.exists:
                        wait(pe, gate_done, m.times(HG, HG))
                        project(work[:, bank0(m, 1)], w0, CH, x).then_inc(k_ps[0], 1)
                    if (s, n) == (1, 0) and nxt.exists:
                        wait(pe, q_done[0], nxt.times(1, 1))
                        project_tokens(work[:, bank0(m, 2)], w0, 2 * CH, x).then_inc(v_ps[0], 1)
                    if (s, n) == (1, 1) and far.exists:
                        wait(pe, g_done[0], far.times(1, 1))
                        wait(pe, k_done[0], nxt.times(1, 1))
                        for tb in range(TB):
                            for cb in range(CB):
                                ins = pe.transpose(work[:, bank0(m, 3), tb, cb * P:(cb + 1) * P],
                                                   g_sb[:, far.base % 2, cb, tb * P:(tb + 1) * P], ident[:])
                        ins.then_inc(t1_done, 1)
                    if (s, n) == (2, 0) and last.exists:
                        wait(pe, att_done[0], last.times(1, 1))
                        if nxt.exists:
                            wait(pe, v_done[0], nxt.times(1, 1))
                        elif m.exists:
                            wait(pe, k_done[0], m.times(1, 1))
                        else:
                            wait(pe, gate_done, last.times(HG, HG))
                        project(work[:, bank0(m, 4)], wf0, 0, att).then_inc(y_ps[0], 1)
                    if (s, n) == (2, 1) and far.exists:
                        wait(pe, xn_done, far.times(TB, TB))
                        for cb in range(CB):
                            for tb in range(TB):
                                ins = pe.transpose(work[:, bank0(m, 5), cb, tb * P:(tb + 1) * P],
                                                   xn[:, tb, cb * P:(cb + 1) * P], ident[:])
                        ins.then_inc(t2_done, 1)
                    if (s, n) == (3, 0) and nxt.exists:
                        if last.exists:
                            wait(pe, y_done[0], last.times(CB, CB))
                        else:
                            wait(pe, v_done[0], nxt.times(1, 1))
                        project(work[:, bank0(m, 6)], w0, 3 * CH, x).then_inc(gate_ps, 1)

                for s in range(STEPS0):
                    r, g = (m, s + 2) if s < 2 else (nxt, s - 2)
                    if r.exists:
                        scores(r, g)
                    if m.exists:
                        turns(s, 0)
                    r, g = (m, s - 1) if s > 0 else (last, STEPS0 - 1)
                    if r.exists:
                        mixes(r, g)
                    task(s, 0)
                    if m.exists:
                        turns(s, 1)
                    task(s, 1)

            over_rows(pe, 2, 1, body0)

            group_sums(1)
            pe.wait_ge(y_done[0], CB * ROWS)
            pe.wait_ge(prob1_clear, 1)

            def body1(m):
                last, nxt, far = m + -1, m + 1, m + 2

                def scores(r, g):
                    wait(pe, q_done[1], r.times(HP, HP))
                    wait(pe, k_done[1], r.times(HP, HP))
                    wait(pe, min_done[1], r.times(4 * HP, 4 * (g + 1 - HP)))
                    for ib in range(TB):
                        j0 = ib * (TOK - WIN)
                        for n, (of_q, of_k) in enumerate(PRODUCTS):
                            for a in range(2):
                                q = slice(a * D1, (a + 1) * D1)
                                ins = pe.matmul(score[:, 2 * g + a, ib, 0:WIN],
                                                nqT[q, r.base % 2, of_q, g, ib * P:(ib + 1) * P],
                                                kT[q, r.base % 2, of_k, g, j0:j0 + WIN],
                                                start=n == 0, stop=n == len(PRODUCTS) - 1)
                                if ib == TB - 1 and n == len(PRODUCTS) - 1:
                                    ins.then_inc(score_done[1], 1)

                def turns(g, a):
                    wait(pe, norm_done[1], m.times(4 * HP, 4 * g + 2 * (a + 1)))
                    if a == 0:
                        wait(pe, turn_done[1][1], m.times(HP, g))
                    else:
                        wait(pe, turn_done[1][0], m.times(HP, g + 1))
                    apart(pe, pe_passed)
                    p = prob1[:, m.base % 2, g, a]
                    pe.transpose(turn[:, P:WIN], p[0:HALO, 1, 0:P], ident[0:HALO, 0:HALO]).then_inc(halo_ps, 1)
                    pe.transpose(turn[:, 0:P], p[:, 0, 0:P], ident[:])
                    pe.transpose(turn[:, WIN + HALO:2 * WIN], p[:, 1, P:TOK], ident[:])
                    wait(pe, halo_ps, m.times(2 * HP, 2 * g + a + 1))
                    apart(pe, pe_passed)
                    pe.transpose(turn[:, WIN:WIN + HALO], p[P - HALO:P, 0, P:TOK], ident[P - HALO:P, P - HALO:P]
                                 ).then_inc(turn_ps[1][a], 1)

                def mixes(r, g):
                    wait(pe, v_done[1], r.times(1, 1))
                    wait(pe, att_done[1], r.times(1, 0))
                    for a in range(2):
                        wait(pe, turn_done[1][a], r.times(HP, g + 1))
                    for jb in range(TB):
                        i0 = jb * (TOK - WIN)
                        for a in range(2):
                            c = (2 * g + a) * D1
                            ins = pe.matmul(mix[a * D1:(a + 1) * D1, g, i0:i0 + WIN], v_sb[:, r.base % 4, jb, c:c + D1],
                                            probT1[:, g, a, jb * WIN:(jb + 1) * WIN], start=jb == 0, stop=jb == TB - 1,
                                            skip_group_check=True)
                    ins.then_inc(mix_ps[1], 1)

                for s in range(HP):
                    if m.exists:
                        turns(s, 0)
                    r, g = (m, s - 1) if s > 0 else (last, HP - 1)
                    if r.exists:
                        mixes(r, g)
                    if s == 0 and nxt.exists:
                        wait(pe, q_done[1], nxt.times(HP, HP))
                        project_tokens(work[:, 0], w1, 2 * CH, src[:, nxt.base % 2]).then_inc(v_ps[1], 1)
                    if s == 1 and far.exists:
                        wait(pe, src_done[1], far.times(1, 1))
                        wait(pe, v_done[1], nxt.times(1, 1))
                        project(work[:, 0], w1, 0, src[:, far.base % 2]).then_inc(q_ps[1], 1)
                    if m.exists:
                        turns(s, 1)
                    if nxt.exists:
                        scores(nxt, s)
                    if s == 0 and last.exists:
                        wait(pe, att_done[1], last.times(1, 1))
                        if nxt.exists:
                            wait(pe, k_done[1], nxt.times(HP, HP))
                        else:
                            wait(pe, y_done[1], last.times(CB, 0))
                        project(work[:, 1], wf1, 0, att).then_inc(y_ps[1], 1)
                    if s == 1 and far.exists:
                        if last.exists:
                            wait(pe, y_done[1], last.times(CB, CB))
                        else:
                            wait(pe, k_done[1], nxt.times(HP, HP))
                        project(work[:, 1], w1, CH, src[:, far.base % 2]).then_inc(k_ps[1], 1)

            over_rows(pe, 2, 1, body1)

        @block.scalar
        def _(act):
            act.wait_ge(consts_in, 16 * 11)
            act.wait_ge(consts_set, 2)
            for w, w_in, scales in weights:
                for cols, scale in scales:
                    act.activation(w[:, HIGH, :, cols], w_in[:, :, cols], ACT.Copy, scale=scale).then_inc(high_set, 1)

            def pair_bias(plus):
                for b in range(2):
                    for ib in range(TB):
                        wait(act, bias_ps, plus(4, 2 * b + ib + 1))
                        apart(act, act_passed)
                        keys = bass.ds(plus(2 * JCHUNK, b * JCHUNK), JCHUNK)
                        act.activation(neg_bias[:, ib, :, keys].rearrange("p h j -> p j h"),
                                       score[:, 2 * b + ib, 0, 0:JCHUNK * H0].rearrange("p (j h) -> p j h", h=H0),
                                       ACT.Copy, scale=-float(D0) ** -0.5).then_inc(bias_done, 1)

            over_chunks(act, NJC, pair_bias)

            def body0(m):
                last, nxt, far = m + -1, m + 1, m + 2

                def exps(r, g, a):
                    for ib in range(TB):
                        wait(act, min_done[0], r.times(4 * STEPS0, 4 * g + 2 * a + ib + 1))
                        act.activation(prob[:, g, a, ib], prob[:, g, a, ib], ACT.Exp, bias=row_min[:, g, a, ib:ib + 1],
                                       scale=-1.0, accum_out=row_sum[:, g, a, ib:ib + 1]).then_inc(exp_done[0], 1)

                for s in range(STEPS0):
                    r, g = (m, s + 2) if s < 2 else (nxt, s - 2)
                    if s == 1 and nxt.exists:
                        wait(act, k_ps[0], nxt.times(1, 1))
                        act.copy(kT[:, nxt.base % 2, HIGH], work[:, bank0(m, 1)]).then_inc(k_high[0], 1)
                    if s == 3 and far.exists:
                        wait(act, t2_done, far.times(1, 1))
                        wait(act, src_done[0], far.times(1, 0))
                        for cb in range(CB):
                            act.activation(xnT[:, cb], work[:, bank0(m, 5), cb], ACT.Identity,
                                           scale=vec0_sb[:, 0, cb:cb + 1], bias=vec0_sb[:, 1, cb:cb + 1]
                                           ).then_inc(xnT_done, 1)
                    if m.exists:
                        wait(act, turn_ps[0][0], m.times(STEPS0, s + 1))
                        wait(act, mix_ps[0], m.times(STEPS0, s - 1))
                        act.copy(probT[:, s % 2, 0], turn[:]).then_inc(turn_done[0][0], 1)
                    if r.exists:
                        exps(r, g, 0)
                    if s == 0 and nxt.exists:
                        wait(act, q_ps[0], nxt.times(1, 1))
                        act.copy(nqT[:, nxt.base % 2, HIGH], work[:, bank0(m, 0)]).then_inc(q_high[0], 1)
                    if s == 0 and last.exists:
                        wait(act, att_sum_done, last.times(1, 1))
                        wait(act, y_ps[0], last.times(1, 0))
                        act.copy(att[:, HIGH], att_sum[:]).then_inc(att_high[0], 1)
                    if s == 1 and nxt.exists:
                        wait(act, v_ps[0], nxt.times(1, 1))
                        act.copy(v_sb[:, nxt.base % 2], work[:, bank0(m, 2)]).then_inc(v_done[0], 1)
                    if r.exists:
                        exps(r, g, 1)
                    if s == 3 and nxt.exists:
                        wait(act, gate_ps, nxt.times(1, 1))
                        wait(act, att_sum_done, nxt.times(1, -1))
                        for hg in range(HG):
                            act.activation(gate[:, nxt.base % 2, hg], work[:, bank0(m, 6), hg], ACT.Tanh, scale=0.5,
                                           bias=half_gate_b[:, hg:hg + 1]).then_inc(gate_done, 1)

            over_rows(act, 2, 1, body0)

            def body1(m):
                last, nxt, far = m + -1, m + 1, m + 2
                def exps(a, s):
                    for ib in range(TB):
                        w = prob1[:, nxt.base % 2, s, a, ib, ib * (TOK - WIN):ib * (TOK - WIN) + WIN]
                        wait(act, min_done[1], nxt.times(4 * HP, 4 * s + 2 * a + ib + 1))
                        act.activation(w, w, ACT.Exp, bias=row_min1[:, nxt.base % 2, s, a, ib:ib + 1], scale=-1.0,
                                       accum_out=row_sum1[:, nxt.base % 2, s, a, ib:ib + 1]).then_inc(exp_done[1], 1)

                for s in range(HP):
                    if s == 0 and nxt.exists:
                        wait(act, k_ps[1], nxt.times(1, 1))
                        for hp in range(HP):
                            act.activation(kT[:, nxt.base % 2, HIGH, hp], work[:, 1, hp], ACT.Identity,
                                           bias=vec1_sb[:, 1, hp:hp + 1]).then_inc(k_high[1], 1)
                    if m.exists:
                        wait(act, turn_ps[1][0], m.times(HP, s + 1))
                        wait(act, mix_ps[1], m.times(HP, s + 1 - HP))
                        act.copy(probT1[:, s, 0], turn[:, 0:2 * WIN]).then_inc(turn_done[1][0], 1)
                    if s == 0 and last.exists:
                        wait(act, mix_ps[1], last.times(HP, HP))
                        wait(act, y_ps[1], last.times(1, 0))
                        act.copy(att[:, HIGH], mix[:]).then_inc(att_high[1], 1)
                    if s == 1 and far.exists:
                        wait(act, q_ps[1], far.times(1, 1))
                        for hp in range(HP):
                            act.activation(nqT[:, far.base % 2, HIGH, hp], work[:, 0, hp], ACT.Identity,
                                           bias=b_q1[:, hp:hp + 1]).then_inc(q_high[1], 1)
                    if nxt.exists:
                        exps(0, s)
                        exps(1, s)

            over_rows(act, 2, 1, body1)

        @block.vector
        def _(dve):
            dve.wait_ge(consts_in, 16 * 11)
            dve.tensor_scalar(half_gate_b[:], vec0_sb[:, 2], 0.5, None, ALU.mult).then_inc(consts_set, 1)
            dve.tensor_scalar(b_q1[:], vec1_sb[:, 0], -float(D1) ** -0.5, None, ALU.mult)
            n = 0
            for w, w_in, scales in weights:
                for cols, scale in scales:
                    n += 1
                    dve.wait_ge(high_set, n)
                    dve.scalar_tensor_tensor(out=w[:, LOW, :, cols], in0=w_in[:, :, cols], scalar=scale,
                                             in1=w[:, HIGH, :, cols].bitcast(F32), op0=ALU.mult, op1=ALU.subtract
                                             ).then_inc(weights_set, 1)
            dve.wait_ge(consts_set, 2)

            def x_stats(plus):
                for b in range(2):
                    wait(dve, x_chunk_in[b], plus(16, 16))
                    apart(dve, dve_passed)
                    for cb in range(CB):
                        for t in range(XCHUNK // 512):
                            at = bass.ds(plus(2 * XCHUNK // 512, b * (XCHUNK // 512) + t), 1)
                            dve.bn_stats(gstat0[:, cb, at], x_chunk[:, b, cb, t * 512:(t + 1) * 512]
                                         ).then_inc(x_chunk_used, 1)

            over_chunks(dve, NXC, x_stats)

            def group_norm(n, stat):
                for cb in range(CB):
                    dve.bn_aggr(ch_mv[:, cb], stat[:, cb].rearrange("p n s -> p (n s)")).then_inc(gn_chain[n], 1)
                dve.wait_ge(gn_ps[n], 1)
                dve.tensor_copy(gn_mean[:], mix[:, 0, 0:CB]).then_inc(gn_chain[n], 1)
                dve.wait_ge(gn_chain[n], 3)
                dve.tensor_tensor(gn_dev[:], ch_mv[:, :, 0], gn_mean[:], ALU.subtract).then_inc(gn_chain[n], 1)
                dve.wait_ge(gn_chain[n], 4)
                dve.tensor_tensor(gn_sq[:], gn_dev[:], gn_dev[:], ALU.mult).then_inc(gn_chain[n], 1)
                dve.wait_ge(gn_chain[n], 5)
                dve.tensor_tensor(gn_sq[:], gn_sq[:], ch_mv[:, :, 1], ALU.add).then_inc(gn_chain[n], 1)
                dve.wait_ge(gn_ps[n], 2)
                dve.tensor_scalar(gn_var[:], mix[:, 0, CB:2 * CB], EPS, None, ALU.add).then_inc(gn_chain[n], 1)
                dve.wait_ge(gn_rstd[n], 1)
                dve.scalar_tensor_tensor(out=gn_shift[n][:], in0=gn_mean[:], scalar=-1.0, in1=gn_scale[n][:],
                                         op0=ALU.mult, op1=ALU.mult).then_inc(gn_ready[n], 1)

            dve.wait_ge(x_chunk_used, XSTATS * NXC)
            group_norm(0, gstat0)
            dve.wait_ge(bias_done, TB * NJC)

            def split(n, m, x):
                dve.tensor_copy(src[:, m.base % 2, HIGH], x).then_inc(src_high[n], 1)
                wait(dve, src_high[n], m.times(1, 1))
                dve.tensor_tensor(src[:, m.base % 2, LOW], x, src[:, m.base % 2, HIGH].bitcast(F32), ALU.subtract
                                  ).then_inc(src_done[n], 1)

            def residual(n, last, bank, bias):
                wait(dve, y_ps[n], last.times(1, 1))
                wait(dve, y_out[n][last.base % 2], last.times(16, 0, of=2))
                for ob in range(CB):
                    dve.scalar_tensor_tensor(out=y_sb[:, last.base % 2, ob], in0=work[:, bank, ob], scalar=bias[:, ob:ob + 1],
                                             in1=x_sb[:, last.base % XSLOTS, ob], op0=ALU.add, op1=ALU.add
                                             ).then_inc(y_done[n], 1)

            def body0(m):
                last, nxt, far = m + -1, m + 1, m + 2

                def mins(r, g, a):
                    wait(dve, score_done[0], r.times(2 * STEPS0, 2 * g + a + 1))
                    wait(dve, turn_ps[0][a], r.times(STEPS0, g + 1 - STEPS0))
                    apart(dve, dve_passed)
                    for ib in range(TB):
                        dve.tensor_tensor_reduce(prob[:, g, a, ib], score[:, (2 * g + a) % HPG, ib],
                                                 neg_bias[:, ib, 2 * g + a], 1.0, 3.0e38, ALU.add, ALU.min,
                                                 row_min[:, g, a, ib:ib + 1]).then_inc(min_done[0], 1)

                for s in range(STEPS0):
                    if s == 1 and nxt.exists:
                        wait(dve, k_high[0], nxt.times(1, 1))
                        dve.tensor_tensor(kT[:, nxt.base % 2, LOW], work[:, bank0(m, 1)],
                                          kT[:, nxt.base % 2, HIGH].bitcast(F32), ALU.subtract).then_inc(k_done[0], 1)
                    r, g = (m, s + 1) if s + 1 < STEPS0 else (nxt, 0)
                    if r.exists:
                        wait(dve, exp_done[0], r.times(4 * STEPS0, 4 * (g + 1)))
                        dve.reciprocal(row_inv[:, g], row_sum[:, g]).then_inc(inv_done[0], 1)
                    if s == 3 and last.exists:
                        residual(0, last, bank0(m, 4), vec0_sb[:, 3])
                        for ob in range(CB):
                            wait(dve, y_done[0], last.times(CB, ob + 1))
                            apart(dve, dve_passed)
                            at = slice(last.base, last.base + 1) if last.loop is None else bass.ds(last.times(1), 1)
                            dve.bn_stats(gstat1[:, ob, at], y_sb[:, last.base % 2, ob]).then_inc(y_stats, 1)
                    r, g = (m, s + 2) if s < 2 else (nxt, s - 2)
                    if r.exists:
                        mins(r, g, 0)
                    if s == 0 and last.exists:
                        wait(dve, mix_ps[0], last.times(STEPS0, STEPS0))
                        wait(dve, gate_done, last.times(HG, HG))
                        wait(dve, att_done[0], last.times(1, 0))
                        dve.scalar_tensor_tensor(out=att_sum[:], in0=gate[:, last.base % 2], scalar=1.0, in1=mix[:],
                                                 op0=ALU.add, op1=ALU.mult).then_inc(att_sum_done, 1)
                    if s == 1 and last.exists:
                        wait(dve, att_high[0], last.times(1, 1))
                        dve.tensor_tensor(att[:, LOW], att_sum[:], att[:, HIGH].bitcast(F32), ALU.subtract
                                          ).then_inc(att_done[0], 1)
                    if s == 2 and far.exists:
                        wait(dve, ln_rstd_done, far.times(1, 1))
                        wait(dve, t2_done, far.times(1, 0))
                        for tb in range(TB):
                            dve.tensor_scalar(xn[:, tb], work[:, bank0(m, 3), tb], ln_mv[:, tb, 0:1],
                                              ln_rstd[:, tb:tb + 1], ALU.subtract, ALU.mult).then_inc(xn_done, 1)
                    if r.exists:
                        mins(r, g, 1)
                    if s == 3 and far.exists:
                        wait(dve, xnT_done, far.times(CB, CB))
                        wait(dve, gate_ps, far.times(1, -1))
                        split(0, far, xnT[:])
                    if m.exists:
                        wait(dve, turn_ps[0][1], m.times(STEPS0, s + 1))
                        wait(dve, mix_ps[0], m.times(STEPS0, s - 1))
                        dve.tensor_copy(probT[:, s % 2, 1], turn[:]).then_inc(turn_done[0][1], 1)
                    if s == 0 and nxt.exists:
                        wait(dve, q_high[0], nxt.times(1, 1))
                        dve.tensor_tensor(nqT[:, nxt.base % 2, LOW], work[:, bank0(m, 0)],
                                          nqT[:, nxt.base % 2, HIGH].bitcast(F32), ALU.subtract).then_inc(q_done[0], 1)
                    if s == 1 and far.exists:
                        wait(dve, t1_done, far.times(1, 1))
                        for tb in range(TB):
                            dve.bn_stats(ln_st[:, tb], work[:, bank0(m, 3), tb]).then_inc(ln_chain, 1)
                        for tb in range(TB):
                            wait(dve, ln_chain, far.times(2 * TB, tb + 1))
                            apart(dve, dve_passed)
                            dve.bn_aggr(ln_mv[:, tb], ln_st[:, tb]).then_inc(ln_chain, 1)
                        wait(dve, ln_chain, far.times(2 * TB, 2 * TB))
                        dve.tensor_scalar(ln_var[:], ln_mv[:, :, 1], EPS, None, ALU.add).then_inc(ln_var_done, 1)

            over_rows(dve, 2, 1, body0)

            dve.wait_ge(y_stats, CB * ROWS)
            group_norm(1, gstat1)
            dve.wait_ge(prob1_clear, 1)

            def body1(m):
                last, nxt, far = m + -1, m + 1, m + 2

                def mins(a, s):
                    wait(dve, score_done[1], nxt.times(2 * HP, 2 * s + a + 1))
                    wait(dve, turn_ps[1][a], nxt.times(HP, s + 1 - 2 * HP))
                    apart(dve, dve_passed)
                    for ib in range(TB):
                        j0 = ib * (TOK - WIN)
                        dve.tensor_tensor_reduce(prob1[:, nxt.base % 2, s, a, ib, j0:j0 + WIN],
                                                 score[:, 2 * s + a, ib, 0:WIN], band[:, ib], 1.0, 3.0e38,
                                                 ALU.add, ALU.min, row_min1[:, nxt.base % 2, s, a, ib:ib + 1]
                                                 ).then_inc(min_done[1], 1)

                def low(r, to, at, bias, done):
                    for hp in range(HP):
                        dve.scalar_tensor_tensor(out=to[:, r.base % 2, LOW, hp], in0=work[:, at, hp],
                                                 scalar=bias[:, hp:hp + 1], in1=to[:, r.base % 2, HIGH, hp].bitcast(F32),
                                                 op0=ALU.add, op1=ALU.subtract).then_inc(done, 1)

                for s in range(HP):
                    if s == 0 and nxt.exists:
                        wait(dve, k_high[1], nxt.times(HP, HP))
                        low(nxt, kT, 1, vec1_sb[:, 1], k_done[1])
                    if s == 1 and last.exists:
                        residual(1, last, 1, vec1_sb[:, 2])
                    r, g = (m, 1) if s == 0 else (nxt, 0)
                    if r.exists:
                        wait(dve, exp_done[1], r.times(4 * HP, 4 * (g + 1)))
                        dve.reciprocal(row_inv1[:, r.base % 2, g], row_sum1[:, r.base % 2, g]).then_inc(inv_done[1], 1)
                    if s == 0 and nxt.exists:
                        wait(dve, v_ps[1], nxt.times(1, 1))
                        dve.tensor_tensor(v_sb[:, nxt.base % 4], work[:, 0], bv1_sb[:].unsqueeze(1).broadcast_to([P, TB, CH]),
                                          ALU.add).then_inc(v_done[1], 1)
                    if s == 0 and last.exists:
                        wait(dve, att_high[1], last.times(1, 1))
                        dve.tensor_tensor(att[:, LOW], mix[:], att[:, HIGH].bitcast(F32), ALU.subtract
                                          ).then_inc(att_done[1], 1)
                    if m.exists:
                        wait(dve, turn_ps[1][1], m.times(HP, s + 1))
                        wait(dve, mix_ps[1], m.times(HP, s + 1 - HP))
                        dve.tensor_copy(probT1[:, s, 1], turn[:, 0:2 * WIN]).then_inc(turn_done[1][1], 1)
                    if nxt.exists:
                        mins(0, s)
                        mins(1, s)
                    if s == 0 and far.exists:
                        wait(dve, g_done[1], far.times(1, 1))
                        wait(dve, v_ps[1], far.times(1, -1))
                        split(1, far, g_sb[:, far.base % 2])
                    if s == 1 and far.exists:
                        wait(dve, q_high[1], far.times(HP, HP))
                        low(far, nqT, 0, b_q1, q_done[1])

            over_rows(dve, 2, 1, body1)


def channels(v):
    return np.asarray(v).reshape(CB, P).T


def rows_first(w, cols):
    return np.ascontiguousarray(np.asarray(w).reshape(CB, P, cols).transpose(1, 0, 2))


def kernel(**inputs):
    import concourse.bacc as bacc
    from concourse.bass_utils import run_bass_kernel_spmd

    a = {k: np.asarray(v) for k, v in inputs.items()}
    xT = np.ascontiguousarray(a["x"][0].transpose(2, 0, 1)).reshape(CH, ROWS * TOK)
    pairT = np.ascontiguousarray(a["L0_conv_x2d"][0].transpose(2, 1, 0))
    qkv = a["L0_conv_qkv_w"].reshape(D0, 3, H0, CH).transpose(3, 1, 2, 0).reshape(CH, 3 * CH)
    gate = a["L0_conv_gate_w"].reshape(D0, H0, CH).transpose(2, 1, 0).reshape(CH, CH)
    gate_b = a["L0_conv_gate_b"].reshape(D0, H0).T.reshape(CH)
    final = a["L0_conv_final_w"].T.reshape(D0, H0, CH).transpose(1, 0, 2).reshape(CH, CH)
    b_in = a["L1_conv_b_in"]

    c = np.arange(P)
    group_mean = np.where(c[:, None] // GROUP == c[None, :] // GROUP, 1.0 / GROUP, 0.0).astype(np.float32)
    queries = c[:, None, None] + P * np.arange(TB)[None, :, None]
    keys = np.arange(WIN)[None, None, :] + (TOK - WIN) * np.arange(TB)[None, :, None]
    band = np.where(abs(queries - keys) <= BAND, 0.0, FAR).astype(np.float32)

    arrays = {
        "xT": xT,
        "pairT": pairT,
        "w0_d": rows_first(np.concatenate([qkv, gate], axis=1), 4 * CH),
        "wf0_d": rows_first(final, CH),
        "pair_w": np.ascontiguousarray(a["L0_conv_x2d_w"].T),
        "vec0": np.ascontiguousarray(np.stack([channels(v) for v in (
            a["L0_conv_norm_w"], a["L0_conv_norm_b"], gate_b, a["L0_conv_final_b"])], axis=1)),
        "w1_d": rows_first(a["L1_conv_w_in"].T, 3 * CH),
        "wf1_d": rows_first(a["L1_conv_w_out"].T, CH),
        "vec1": np.ascontiguousarray(np.stack([channels(v) for v in (
            b_in[:CH], b_in[CH:2 * CH], a["L1_conv_b_out"])], axis=1)),
        "bv1": np.ascontiguousarray(b_in[2 * CH:].reshape(1, CH)),
        "ident_d": np.eye(P, dtype=np.float32),
        "group_d": group_mean,
        "band_d": band,
    }
    nc = bacc.Bacc("TRN2", target_bir_lowering=False, num_devices=1)
    aps = {n: nc.dram_tensor(n, v.shape, F32, kind="ExternalInput").ap() for n, v in arrays.items()}
    aps["x1T"] = nc.dram_tensor("x1T", (CH, ROWS * TOK), F32, kind="Internal").ap()
    aps["outT"] = nc.dram_tensor("outT", (CH, ROWS * TOK), F32, kind="ExternalOutput").ap()
    conv_preact_kernel(nc, **aps)
    r = run_bass_kernel_spmd(nc, [arrays], core_ids=[0])
    out = r.results[0]["outT"].reshape(CH, ROWS, TOK).transpose(1, 2, 0)
    return np.ascontiguousarray(out).reshape(1, ROWS, TOK, CH)
```

```python
from contextlib import ExitStack

import numpy as np

import concourse.bass as bass
from concourse import mybir

F32 = mybir.dt.float32
F32R = mybir.dt.float32r
ALU = mybir.AluOpType
ACT = mybir.ActivationFunctionType

P = 128
ROWS, TOK, CH = 128, 256, 256
CB = CH // P
TB = TOK // P
GROUP = CH // 32
EPS = 1e-5

H0, D0 = 8, 32
HG = H0 * D0 // P
HPG = P // D0
STEPS0 = H0 // 2
PAIR = 128

H1, D1 = 4, 64
HP = H1 // 2
BAND = 16
HALO = 32
WIN = P + HALO
SPAN = slice(P - HALO, P - HALO + 2 * WIN)
FAR = 1.0e30

HIGH, LOW = 0, 1
PRODUCTS = ((HIGH, HIGH), (LOW, HIGH), (HIGH, LOW))

UNROLL = 4
XSLOTS = 4

XCHUNK = 1024
QUAD = 32
JCHUNK = 2 * P // QUAD


class Row:

    def __init__(self, loop, base):
        self.loop, self.base = loop, base

    def __add__(self, n):
        return Row(self.loop, self.base + n)

    @property
    def exists(self):
        return self.loop is not None or 0 <= self.base < ROWS

    def times(self, per, plus=0, of=1):
        fixed = per * (self.base // of) + plus
        return fixed if self.loop is None else self.loop * (per * UNROLL // of) + fixed

    def tokens(self):
        return bass.ds(self.times(TOK), TOK)


def wait(eng, sem, value):
    if isinstance(value, int):
        if value > 0:
            eng.wait_ge(sem, value)
    else:
        eng.wait_ge(sem, value)


def over_rows(eng, before, after, body):
    for m in range(-before, UNROLL):
        body(Row(None, m))
    with eng.Fori(0, ROWS // UNROLL - 2) as i:
        for k in range(UNROLL):
            body(Row(i, UNROLL + k))
    for m in range(ROWS - UNROLL, ROWS + after):
        body(Row(None, m))


def over_chunks(eng, count, body):
    body(lambda per, fixed: fixed, True)
    with eng.Fori(0, count // 2 - 2) as i:
        body(lambda per, fixed: i * per + (per + fixed), True)
    body(lambda per, fixed: (count // 2 - 1) * per + fixed, False)


def conv_preact_kernel(nc, xT, x_nat, pairT, w0_d, wf0_d, pair_w, vec0, w1_d, wf1_d, vec1, bv1,
                       ident_d, group_d, band_d, x1T, outT):
    x_v = xT.rearrange("(c p) t -> p c t", p=P)
    x_tok_v = x_nat.rearrange("(b p) c -> p b c", p=P)
    x1_v = x1T.rearrange("(c p) t -> p c t", p=P)
    out_v = outT.rearrange("(c p) t -> p c t", p=P)

    with ExitStack() as ctx:
        def sb(name, shape, dt=F32):
            return ctx.enter_context(nc.sbuf_tensor(name, shape, dt))

        def sem(name):
            return ctx.enter_context(nc.semaphore(name))

        ident = sb("ident", [P, P])
        group_mean = sb("group_mean", [P, P])
        band = sb("band", [P, TB, WIN])
        w0 = sb("w0", [P, 2, CB, 4 * CH], F32R)
        wf0 = sb("wf0", [P, 2, CB, CH], F32R)
        pairw_sb = sb("pairw_sb", [P, QUAD])
        vec0_sb = sb("vec0_sb", [P, 4, CB])
        w1 = sb("w1", [P, 2, CB, 3 * CH], F32R)
        wf1 = sb("wf1", [P, 2, CB, CH], F32R)
        vec1_sb = sb("vec1_sb", [P, 3, CB])
        bv1_sb = sb("bv1_sb", [P, CH])
        minus_half = sb("minus_half", [P, CB])
        half_gate_b = sb("half_gate_b", [P, CB])
        b_q1 = sb("b_q1", [P, CB])
        gstat0 = sb("gstat0", [P, CB, ROWS * TOK // 512, 6])
        gstat1 = sb("gstat1", [P, CB, ROWS, 6])
        ch_mv = sb("ch_mv", [P, CB, 2])
        gn_mean = sb("gn_mean", [P, CB])
        gn_dev = sb("gn_dev", [P, CB])
        gn_sq = sb("gn_sq", [P, CB])
        gn_var = sb("gn_var", [P, CB])
        gn_scale = [sb(f"gn_scale{n}", [P, CB]) for n in range(2)]
        gn_shift = [sb(f"gn_shift{n}", [P, CB]) for n in range(2)]
        ones = sb("ones", [P, P])
        gn_diag = sb("gn_diag", [P, 2, CB, P])
        gn_row = sb("gn_row", [P, 2, CH])
        x_chunk = sb("x_chunk", [P, 2, CB, XCHUNK])
        pair_chunk = sb("pair_chunk", [P, 2, JCHUNK, TOK])
        bias_rows = sb("bias_rows", [P, 2, 2 * TOK])
        neg_bias = sb("neg_bias", [P, TB, H0, TOK])
        x_sb = sb("x_sb", [P, XSLOTS, CB, TOK])
        x_tok = sb("x_tok", [P, 2, TB, CH])
        g_tok = sb("g_tok", [P, 2, TB, CH])
        g_sb = g_tok[:].rearrange("p r b c -> p r (b c)").rearrange("p r (c t) -> p r c t", c=CB)
        ln_st = sb("ln_st", [P, TB, 6])
        ln_mv = sb("ln_mv", [P, TB, 2])
        ln_var = sb("ln_var", [P, TB])
        ln_rstd = sb("ln_rstd", [P, TB])
        xn = sb("xn", [P, TB, CH])
        xnT = sb("xnT", [P, CB, TOK])
        src = sb("src", [P, 2, 2, CB, TOK], F32R)
        nqT = sb("nqT", [P, 2, 2, CB, TOK], F32R)
        kT = sb("kT", [P, 2, 2, CB, TOK], F32R)
        v_sb = sb("v_sb", [P, 4, TB, CH])
        gate = sb("gate", [P, 2, HG, TOK])
        prob = sb("prob", [P, STEPS0, 2, TB, TOK])
        row_min = sb("row_min", [P, STEPS0, 2, TB])
        row_sum = sb("row_sum", [P, STEPS0, 2, TB])
        row_inv = sb("row_inv", [P, STEPS0, 2, TB])
        probT = sb("probT", [P, 2, 2, TB, TOK])
        att_sum = sb("att_sum", [P, HG, TOK])
        att = sb("att", [P, 2, HG, TOK], F32R)
        y_sb = sb("y_sb", [P, 2, CB, TOK])
        prob1 = prob[:].rearrange("p (r g) a b t -> p r g a b t", r=2)
        row_min1 = sb("row_min1", [P, 2, HP, 2, TB])
        row_sum1 = sb("row_sum1", [P, 2, HP, 2, TB])
        row_inv1 = sb("row_inv1", [P, 2, HP, 2, TB])
        probT1 = probT[:].rearrange("p s a b t -> p s a (b t)")[:, :, :, 0:2 * WIN]
        stage = prob[:].rearrange("p g a b t -> p (g a b t)")
        sizes = (4 * CH, CH, 3 * CH)
        starts = (0, CB * 4 * CH, CB * 5 * CH)
        w0_in, wf0_in, w1_in = (stage[:, s0:s0 + CB * n].rearrange("p (c n) -> p c n", c=CB)
                                for s0, n in zip(starts, sizes))
        wf1_in = probT[:].rearrange("p s a b t -> p (s a b t)")[:, 0:CB * CH].rearrange("p (c n) -> p c n", c=CB)

        score = ctx.enter_context(nc.psum_tensor("score", [P, 4, TB, TOK], F32))
        turn = ctx.enter_context(nc.psum_tensor("turn", [P, 2 * TOK], F32))
        mix = ctx.enter_context(nc.psum_tensor("mix", [P, 2, TOK], F32))
        work = ctx.enter_context(nc.psum_tensor("work", [P, 2, 2, TOK], F32))

        consts_in = sem("consts_in")
        consts_set = sem("consts_set")
        pairw_clear = sem("pairw_clear")
        high_set = sem("high_set")
        weights_set = sem("weights_set")
        x_chunk_in = [sem(f"x_chunk_in{n}") for n in range(2)]
        x_chunk_used = sem("x_chunk_used")
        pair_in = [sem(f"pair_in{n}") for n in range(2)]
        bias_ps = sem("bias_ps")
        bias_copied = sem("bias_copied")
        bias_turned = sem("bias_turned")
        bias_done = sem("bias_done")
        gn_chain = [sem(f"gn_chain{n}") for n in range(2)]
        gn_ps = [sem(f"gn_ps{n}") for n in range(2)]
        gn_rstd = [sem(f"gn_rstd{n}") for n in range(2)]
        gn_ready = [sem(f"gn_ready{n}") for n in range(2)]

        x_in = [[sem(f"x_in{n}_{s}") for s in range(XSLOTS)] for n in range(2)]
        g_done = [sem(f"g_done{n}") for n in range(2)]
        x_tok_in = [sem(f"x_tok_in{s}") for s in range(2)]
        gn_scaled = sem("gn_scaled")
        gn_diag_set = sem("gn_diag_set")
        gn_row_ps = sem("gn_row_ps")
        gn_row_done = sem("gn_row_done")
        ln_chain = sem("ln_chain")
        ln_var_done = sem("ln_var_done")
        ln_rstd_done = sem("ln_rstd_done")
        xn_done = sem("xn_done")
        t2_done = sem("t2_done")
        xnT_done = sem("xnT_done")
        q_ps = [sem(f"q_ps{n}") for n in range(2)]
        k_ps = [sem(f"k_ps{n}") for n in range(2)]
        v_ps = [sem(f"v_ps{n}") for n in range(2)]
        gate_ps = sem("gate_ps")
        y_ps = [sem(f"y_ps{n}") for n in range(2)]
        src_high = [sem(f"src_high{n}") for n in range(2)]
        src_done = [sem(f"src_done{n}") for n in range(2)]
        q_high = [sem(f"q_high{n}") for n in range(2)]
        k_high = [sem(f"k_high{n}") for n in range(2)]
        att_sum_done = sem("att_sum_done")
        att_high = [sem(f"att_high{n}") for n in range(2)]
        q_done = [sem(f"q_done{n}") for n in range(2)]
        k_done = [sem(f"k_done{n}") for n in range(2)]
        v_done = [sem(f"v_done{n}") for n in range(2)]
        gate_done = sem("gate_done")
        y_done = [sem(f"y_done{n}") for n in range(2)]
        y_stats = sem("y_stats")
        score_done = [sem(f"score_done{n}") for n in range(2)]
        min_done = [sem(f"min_done{n}") for n in range(2)]
        exp_done = [sem(f"exp_done{n}") for n in range(2)]
        inv_done = [sem(f"inv_done{n}") for n in range(2)]
        norm_done = [sem(f"norm_done{n}") for n in range(2)]
        turn_ps = [[sem(f"turn_ps{n}_{a}") for a in range(2)] for n in range(2)]
        turn_done = [[sem(f"turn_done{n}_{a}") for a in range(2)] for n in range(2)]
        mix_ps = [sem(f"mix_ps{n}") for n in range(2)]
        att_done = [sem(f"att_done{n}") for n in range(2)]
        prob1_clear = sem("prob1_clear")
        y_out = [[sem(f"y_out{n}_{s}") for s in range(2)] for n in range(2)]

        NXC = ROWS * TOK // XCHUNK
        XSTATS = CB * XCHUNK // 512
        NJC = TOK // JCHUNK

        pool_passed, act_passed, dve_passed, sp_passed, pe_passed = (
            sem(f"{e}_passed") for e in ("pool", "act", "dve", "sp", "pe"))

        def apart(eng, passed):
            eng.sem_inc(passed, 1)

        everything = slice(0, CH)
        weights = ((w0, w0_in, ((everything, -1.0), (slice(CH, 4 * CH), 1.0))),
                   (wf0, wf0_in, ((everything, 0.5),)),
                   (w1, w1_in, ((everything, -float(D1) ** -0.5), (slice(CH, 3 * CH), 1.0))),
                   (wf1, wf1_in, ((everything, 1.0),)))

        block = ctx.enter_context(nc.Block())

        @block.sync
        def _(sp):
            sp.wait_ge(pairw_clear, 1)
            for to, of in ((w0_in, w0_d), (wf0_in, wf0_d), (w1_in, w1_d), (wf1_in, wf1_d), (ident[:], ident_d),
                           (group_mean[:], group_d), (band[:], band_d), (pairw_sb[:, 0:H0], pair_w), (vec0_sb[:], vec0),
                           (vec1_sb[:], vec1)):
                sp.dma_start(to, of).then_inc(consts_in, 16)
            sp.dma_start(bv1_sb[:], bv1.broadcast_to([P, CH])).then_inc(consts_in, 16)

            def chunks(plus, more):
                for b in range(2):
                    wait(sp, x_chunk_used, plus(2 * XSTATS, XSTATS * (b - 1)))
                    apart(sp, sp_passed)
                    sp.dma_start(x_chunk[:, b], x_v[:, :, bass.ds(plus(2 * XCHUNK, b * XCHUNK), XCHUNK)]
                                 ).then_inc(x_chunk_in[b], 16)

            over_chunks(sp, NXC, chunks)

            def rows(n, of, to):
                def body(m):
                    if (m + -1).exists:
                        wait(sp, y_done[n], m.times(CB))
                        apart(sp, sp_passed)
                        sp.dma_start(to[:, :, (m + -1).tokens()], y_sb[:, (m.base - 1) % 2]
                                     ).then_inc(y_out[n][(m.base - 1) % 2], 16)
                    if (m + 3).exists and (m.loop is not None or m.base + 3 < ROWS):
                        slot = (m.base + 3) % XSLOTS
                        sp.dma_start(x_sb[:, slot], of[:, :, (m + 3).tokens()]).then_inc(x_in[n][slot], 16)
                        if n == 0:
                            wait(sp, g_done[0], (m + 3).times(1, -1))
                            apart(sp, sp_passed)
                            sp.dma_start(x_tok[:, (m.base + 3) % 2], x_tok_v[:, bass.ds((m + 3).times(TB), TB), :]
                                         ).then_inc(x_tok_in[(m.base + 3) % 2], 16)

                over_rows(sp, 3, 1, body)
                for s in range(2):
                    sp.wait_ge(y_out[n][s], 16 * ROWS // 2)

            rows(0, x_v, x1_v)
            rows(1, x1_v, out_v)

        @block.gpsimd
        def _(pool):
            pool.memset(pairw_sb[:], 0.0).then_inc(pairw_clear, 1)
            pool.memset(ones[:], 1.0)
            pool.memset(minus_half[:], -0.5).then_inc(consts_set, 1)

            def power(n):
                pool.wait_ge(consts_set, 2)
                pool.wait_ge(gn_chain[n], 7)
                pool.tensor_tensor(gn_scale[n][:], gn_var[:], minus_half[:], ALU.pow).then_inc(gn_rstd[n], 1)
                pool.wait_ge(gn_ready[n], 1)

            power(0)
            pool.wait_ge(gn_row_done, 1)

            def body0(m):
                for s in range(STEPS0):
                    r, g = (m, s + 1) if s + 1 < STEPS0 else (m + 1, 0)
                    if r.exists:
                        wait(pool, inv_done[0], r.times(STEPS0, g + 1))
                        apart(pool, pool_passed)
                        for a in range(2):
                            for ib in range(TB):
                                pool.tensor_scalar(prob[:, g, a, ib], prob[:, g, a, ib], row_inv[:, g, a, ib:ib + 1],
                                                   1.0, ALU.mult, ALU.mult).then_inc(norm_done[0], 1)
                    if s == 0 and (m + 2).exists:
                        wait(pool, x_tok_in[m.base % 2], (m + 2).times(16, 16, of=2))
                        wait(pool, xn_done, m.times(TB, TB))
                        apart(pool, pool_passed)
                        g = g_tok[:, m.base % 2]
                        pool.tensor_tensor(g, x_tok[:, m.base % 2], gn_row[:, 0].unsqueeze(1).broadcast_to([P, TB, CH]),
                                           ALU.mult).then_inc(gn_scaled, 1)
                        wait(pool, gn_scaled, (m + 2).times(1, 1))
                        pool.tensor_tensor(g, g, gn_row[:, 1].unsqueeze(1).broadcast_to([P, TB, CH]), ALU.add
                                           ).then_inc(g_done[0], 1)
                    if s == 1 and (m + 2).exists:
                        wait(pool, ln_var_done, (m + 2).times(1, 1))
                        apart(pool, pool_passed)
                        pool.tensor_tensor(ln_rstd[:], ln_var[:], minus_half[:], ALU.pow).then_inc(ln_rstd_done, 1)

            over_rows(pool, 2, 0, body0)

            pool.wait_ge(turn_ps[0][1], STEPS0 * ROWS)
            pool.memset(prob[:], 0.0).then_inc(prob1_clear, 1)
            power(1)

            def body1(m):
                for s in range(HP):
                    if s == 0 and (m + 2).exists:
                        wait(pool, x_in[1][(m.base + 2) % XSLOTS], (m + 2).times(16, 16, of=XSLOTS))
                        wait(pool, src_done[1], (m + 2).times(1, -1))
                        apart(pool, pool_passed)
                        for cb in range(CB):
                            ins = pool.tensor_scalar(g_sb[:, m.base % 2, cb], x_sb[:, (m.base + 2) % XSLOTS, cb],
                                                     gn_scale[1][:, cb:cb + 1], gn_shift[1][:, cb:cb + 1],
                                                     ALU.mult, ALU.add)
                        ins.then_inc(g_done[1], 1)
                    r, g = (m, 1) if s == 0 else (m + 1, 0)
                    if r.exists:
                        wait(pool, inv_done[1], r.times(HP, g + 1))
                        apart(pool, pool_passed)
                        for a in range(2):
                            for ib in range(TB):
                                w = prob1[:, r.base % 2, g, a, ib, ib * (TOK - WIN):ib * (TOK - WIN) + WIN]
                                pool.tensor_scalar(w, w, row_inv1[:, r.base % 2, g, a, ib:ib + 1], 1.0,
                                                   ALU.mult, ALU.mult).then_inc(norm_done[1], 1)

            over_rows(pool, 2, 0, body1)

        @block.tensor
        def _(pe):
            pe.wait_ge(consts_in, 16 * 11)
            def pair_bias(plus, more):
                for b in range(2):
                    wait(pe, pair_in[b], plus(16, 16))
                    wait(pe, bias_copied, plus(2, b - 1))
                    for n in range(P // QUAD):
                        ins = pe.matmul(score[n * QUAD:(n + 1) * QUAD, b].rearrange("p b t -> p (b t)"), pairw_sb[:],
                                        pair_chunk[:, b, 2 * n:2 * n + 2].rearrange("p j t -> p (j t)"),
                                        start=True, stop=True, skip_group_check=True)
                    ins.then_inc(bias_ps, 1)
                    wait(pe, bias_copied, plus(2, b + 1))
                    wait(pe, bias_done, plus(4, 2 * b - 2))
                    for n in range(2 * TB):
                        ins = pe.transpose(score[:, 2 + b, n // TB, n % TB * P:(n % TB + 1) * P],
                                           bias_rows[:, b, n * P:(n + 1) * P], ident[:])
                    ins.then_inc(bias_turned, 1)

            over_chunks(pe, NJC, pair_bias)

            def group_sums(n):
                pe.wait_ge(gn_chain[n], 2)
                pe.matmul(mix[:, 0, 0:CB], group_mean[:], ch_mv[:, :, 0], start=True, stop=True).then_inc(gn_ps[n], 1)
                pe.wait_ge(gn_chain[n], 6)
                pe.matmul(mix[:, 0, CB:2 * CB], group_mean[:], gn_sq[:], start=True, stop=True).then_inc(gn_ps[n], 1)

            group_sums(0)
            pe.wait_ge(gn_diag_set, 2 * CB)
            pe.matmul(turn[:], ones[:], gn_diag[:].rearrange("p n c q -> p (n c q)"), start=True, stop=True
                      ).then_inc(gn_row_ps, 1)
            pe.wait_ge(weights_set, sum(len(scales) for _, _, scales in weights))

            def project(out, w, cols, x):
                for cb in range(CB):
                    terms = [(kb, part) for kb in range(CB) for part in PRODUCTS]
                    for n, (kb, (of_w, of_x)) in enumerate(terms):
                        ins = pe.matmul(out[:, cb], w[:, of_w, kb, cols + cb * P:cols + (cb + 1) * P], x[:, of_x, kb],
                                        start=n == 0, stop=n == len(terms) - 1)
                return ins

            def project_tokens(out, w, cols, x):
                for tb in range(TB):
                    terms = [(kb, part) for kb in range(CB) for part in PRODUCTS]
                    for n, (kb, (of_w, of_x)) in enumerate(terms):
                        ins = pe.matmul(out[:, tb], x[:, of_x, kb, tb * P:(tb + 1) * P], w[:, of_w, kb, cols:cols + CH],
                                        start=n == 0, stop=n == len(terms) - 1)
                return ins

            def body0(m):
                last, nxt, far = m + -1, m + 1, m + 2
                x = src[:, nxt.base % 2]

                def scores(r, g):
                    wait(pe, q_done[0], r.times(1, 1))
                    wait(pe, k_done[0], r.times(1, 1))
                    wait(pe, min_done[0], r.times(4 * STEPS0, 4 * (g - 1)))
                    for ib in range(TB):
                        for n, (of_q, of_k) in enumerate(PRODUCTS):
                            for a in range(2):
                                hg, h = divmod(2 * g + a, HPG)
                                q = slice(h * D0, (h + 1) * D0)
                                ins = pe.matmul(score[:, h, ib], nqT[q, r.base % 2, of_q, hg, ib * P:(ib + 1) * P],
                                                kT[q, r.base % 2, of_k, hg], start=n == 0, stop=n == len(PRODUCTS) - 1)
                                if ib == TB - 1 and n == len(PRODUCTS) - 1:
                                    ins.then_inc(score_done[0], 1)

                def turns(g, a):
                    wait(pe, norm_done[0], m.times(4 * STEPS0, 4 * g + 2 * (a + 1)))
                    if a == 0:
                        wait(pe, turn_done[0][1], m.times(STEPS0, g))
                    else:
                        wait(pe, turn_done[0][0], m.times(STEPS0, g + 1))
                    for jb in range(TB):
                        for ib in range(TB):
                            ins = pe.transpose(turn[:, jb * TOK + ib * P:jb * TOK + (ib + 1) * P],
                                               prob[:, g, a, ib, jb * P:(jb + 1) * P], ident[:])
                    ins.then_inc(turn_ps[0][a], 1)

                def mixes(r, g):
                    wait(pe, v_done[0], r.times(1, 1))
                    wait(pe, att_sum_done, r.times(1, 0))
                    for a in range(2):
                        wait(pe, turn_done[0][a], r.times(STEPS0, g + 1))
                    for jb in range(TB):
                        for a in range(2):
                            hg, h = divmod(2 * g + a, HPG)
                            c = (2 * g + a) * D0
                            ins = pe.matmul(mix[h * D0:(h + 1) * D0, hg], v_sb[:, r.base % 2, jb, c:c + D0],
                                            probT[:, g % 2, a, jb], start=jb == 0, stop=jb == TB - 1,
                                            skip_group_check=True)
                    ins.then_inc(mix_ps[0], 1)

                def task(s, n):
                    if (s, n) == (0, 0) and nxt.exists:
                        wait(pe, src_done[0], nxt.times(1, 1))
                        project(work[:, 0], w0, 0, x).then_inc(q_ps[0], 1)
                    if (s, n) == (0, 1) and nxt.exists:
                        wait(pe, gate_done, m.times(HG, HG))
                        project(work[:, 1], w0, CH, x).then_inc(k_ps[0], 1)
                    if (s, n) == (1, 0) and nxt.exists:
                        wait(pe, q_done[0], nxt.times(1, 1))
                        project_tokens(work[:, 0], w0, 2 * CH, x).then_inc(v_ps[0], 1)
                    if (s, n) == (2, 0) and last.exists:
                        wait(pe, att_done[0], last.times(1, 1))
                        if nxt.exists:
                            wait(pe, k_done[0], nxt.times(1, 1))
                        elif m.exists:
                            wait(pe, gate_done, m.times(HG, HG))
                        else:
                            wait(pe, y_done[0], last.times(CB, 0))
                        project(work[:, 1], wf0, 0, att).then_inc(y_ps[0], 1)
                    if (s, n) == (2, 1) and far.exists:
                        wait(pe, xn_done, far.times(TB, TB))
                        wait(pe, v_done[0], nxt.times(1, 1))
                        for cb in range(CB):
                            for tb in range(TB):
                                ins = pe.transpose(work[:, 0, cb, tb * P:(tb + 1) * P],
                                                   xn[:, tb, cb * P:(cb + 1) * P], ident[:])
                        ins.then_inc(t2_done, 1)
                    if (s, n) == (3, 0) and nxt.exists:
                        if last.exists:
                            wait(pe, y_done[0], last.times(CB, CB))
                        else:
                            wait(pe, k_done[0], nxt.times(1, 1))
                        project(work[:, 1], w0, 3 * CH, x).then_inc(gate_ps, 1)

                for s in range(STEPS0):
                    r, g = (m, s + 2) if s < 2 else (nxt, s - 2)
                    if r.exists:
                        scores(r, g)
                    if m.exists:
                        turns(s, 0)
                    r, g = (m, s - 1) if s > 0 else (last, STEPS0 - 1)
                    if r.exists:
                        mixes(r, g)
                    task(s, 0)
                    if m.exists:
                        turns(s, 1)
                    task(s, 1)

            over_rows(pe, 2, 1, body0)

            group_sums(1)
            pe.wait_ge(y_done[0], CB * ROWS)
            pe.wait_ge(prob1_clear, 1)

            def body1(m):
                last, nxt, far = m + -1, m + 1, m + 2

                def scores(r, g):
                    wait(pe, q_done[1], r.times(HP, HP))
                    wait(pe, k_done[1], r.times(HP, HP))
                    wait(pe, min_done[1], r.times(4 * HP, 4 * (g + 1 - HP)))
                    for ib in range(TB):
                        j0 = ib * (TOK - WIN)
                        for n, (of_q, of_k) in enumerate(PRODUCTS):
                            for a in range(2):
                                q = slice(a * D1, (a + 1) * D1)
                                ins = pe.matmul(score[:, 2 * g + a, ib, 0:WIN],
                                                nqT[q, r.base % 2, of_q, g, ib * P:(ib + 1) * P],
                                                kT[q, r.base % 2, of_k, g, j0:j0 + WIN],
                                                start=n == 0, stop=n == len(PRODUCTS) - 1)
                                if ib == TB - 1 and n == len(PRODUCTS) - 1:
                                    ins.then_inc(score_done[1], 1)

                def turns(g, a):
                    wait(pe, norm_done[1], m.times(4 * HP, 4 * g + 2 * (a + 1)))
                    if a == 0:
                        wait(pe, turn_done[1][1], m.times(HP, g))
                    else:
                        wait(pe, turn_done[1][0], m.times(HP, g + 1))
                    apart(pe, pe_passed)
                    for n, (jb, ib) in enumerate(((1, 0), (1, 1), (0, 0), (0, 1))):
                        ins = pe.transpose(turn[:, n * P:(n + 1) * P], prob1[:, m.base % 2, g, a, ib, jb * P:(jb + 1) * P],
                                           ident[:])
                    ins.then_inc(turn_ps[1][a], 1)

                def mixes(r, g):
                    wait(pe, v_done[1], r.times(1, 1))
                    wait(pe, att_done[1], r.times(1, 0))
                    for a in range(2):
                        wait(pe, turn_done[1][a], r.times(HP, g + 1))
                    for jb in range(TB):
                        i0 = jb * (TOK - WIN)
                        for a in range(2):
                            c = (2 * g + a) * D1
                            ins = pe.matmul(mix[a * D1:(a + 1) * D1, g, i0:i0 + WIN], v_sb[:, r.base % 4, jb, c:c + D1],
                                            probT1[:, g, a, (1 - jb) * WIN:(2 - jb) * WIN], start=jb == 0, stop=jb == TB - 1,
                                            skip_group_check=True)
                    ins.then_inc(mix_ps[1], 1)

                for s in range(HP):
                    if m.exists:
                        turns(s, 0)
                    r, g = (m, s - 1) if s > 0 else (last, HP - 1)
                    if r.exists:
                        mixes(r, g)
                    if s == 0 and nxt.exists:
                        wait(pe, q_done[1], nxt.times(HP, HP))
                        project_tokens(work[:, 0], w1, 2 * CH, src[:, nxt.base % 2]).then_inc(v_ps[1], 1)
                    if s == 1 and far.exists:
                        wait(pe, src_done[1], far.times(1, 1))
                        wait(pe, v_done[1], nxt.times(1, 1))
                        project(work[:, 0], w1, 0, src[:, far.base % 2]).then_inc(q_ps[1], 1)
                    if m.exists:
                        turns(s, 1)
                    if nxt.exists:
                        scores(nxt, s)
                    if s == 0 and last.exists:
                        wait(pe, att_done[1], last.times(1, 1))
                        if nxt.exists:
                            wait(pe, k_done[1], nxt.times(HP, HP))
                        else:
                            wait(pe, y_done[1], last.times(CB, 0))
                        project(work[:, 1], wf1, 0, att).then_inc(y_ps[1], 1)
                    if s == 1 and far.exists:
                        if last.exists:
                            wait(pe, y_done[1], last.times(CB, CB))
                        else:
                            wait(pe, k_done[1], nxt.times(HP, HP))
                        project(work[:, 1], w1, CH, src[:, far.base % 2]).then_inc(k_ps[1], 1)

            over_rows(pe, 2, 1, body1)

        @block.scalar
        def _(act):
            for b in range(2):
                act.dma_start(pair_chunk[:, b], pairT[:, b * JCHUNK:(b + 1) * JCHUNK, :]).then_inc(pair_in[b], 16)
            act.wait_ge(consts_in, 16 * 11)
            act.wait_ge(consts_set, 2)
            for w, w_in, scales in weights:
                for cols, scale in scales:
                    act.activation(w[:, HIGH, :, cols], w_in[:, :, cols], ACT.Copy, scale=scale).then_inc(high_set, 1)

            def pair_bias(plus, more):
                for b in range(2):
                    wait(act, bias_ps, plus(2, b + 1))
                    apart(act, act_passed)
                    if more:
                        act.dma_start(pair_chunk[:, b], pairT[:, bass.ds(plus(2 * JCHUNK, (b + 2) * JCHUNK), JCHUNK), :]
                                      ).then_inc(pair_in[b], 16)
                    wait(act, bias_turned, plus(2, b - 1))
                    act.activation(bias_rows[:, b], score[:, b].rearrange("p b t -> p (b t)"), ACT.Copy,
                                   scale=-float(D0) ** -0.5).then_inc(bias_copied, 1)

            over_chunks(act, NJC, pair_bias)

            def body0(m):
                last, nxt, far = m + -1, m + 1, m + 2

                def exps(r, g, a):
                    for ib in range(TB):
                        wait(act, min_done[0], r.times(4 * STEPS0, 4 * g + 2 * a + ib + 1))
                        act.activation(prob[:, g, a, ib], prob[:, g, a, ib], ACT.Exp, bias=row_min[:, g, a, ib:ib + 1],
                                       scale=-1.0, accum_out=row_sum[:, g, a, ib:ib + 1]).then_inc(exp_done[0], 1)

                for s in range(STEPS0):
                    r, g = (m, s + 2) if s < 2 else (nxt, s - 2)
                    if s == 1 and nxt.exists:
                        wait(act, k_ps[0], nxt.times(1, 1))
                        act.copy(kT[:, nxt.base % 2, HIGH], work[:, 1]).then_inc(k_high[0], 1)
                    if s == 3 and far.exists:
                        wait(act, t2_done, far.times(1, 1))
                        wait(act, src_done[0], far.times(1, 0))
                        for cb in range(CB):
                            act.activation(xnT[:, cb], work[:, 0, cb], ACT.Identity,
                                           scale=vec0_sb[:, 0, cb:cb + 1], bias=vec0_sb[:, 1, cb:cb + 1]
                                           ).then_inc(xnT_done, 1)
                    if m.exists:
                        wait(act, turn_ps[0][0], m.times(STEPS0, s + 1))
                        wait(act, mix_ps[0], m.times(STEPS0, s - 1))
                        act.copy(probT[:, s % 2, 0], turn[:]).then_inc(turn_done[0][0], 1)
                    if r.exists:
                        exps(r, g, 0)
                    if s == 0 and nxt.exists:
                        wait(act, q_ps[0], nxt.times(1, 1))
                        act.copy(nqT[:, nxt.base % 2, HIGH], work[:, 0]).then_inc(q_high[0], 1)
                    if s == 0 and last.exists:
                        wait(act, att_sum_done, last.times(1, 1))
                        wait(act, y_ps[0], last.times(1, 0))
                        act.copy(att[:, HIGH], att_sum[:]).then_inc(att_high[0], 1)
                    if s == 1 and nxt.exists:
                        wait(act, v_ps[0], nxt.times(1, 1))
                        act.copy(v_sb[:, nxt.base % 2], work[:, 0]).then_inc(v_done[0], 1)
                    if r.exists:
                        exps(r, g, 1)
                    if s == 3 and nxt.exists:
                        wait(act, gate_ps, nxt.times(1, 1))
                        wait(act, att_sum_done, nxt.times(1, -1))
                        for hg in range(HG):
                            act.activation(gate[:, nxt.base % 2, hg], work[:, 1, hg], ACT.Tanh, scale=0.5,
                                           bias=half_gate_b[:, hg:hg + 1]).then_inc(gate_done, 1)

            over_rows(act, 2, 1, body0)

            def body1(m):
                last, nxt, far = m + -1, m + 1, m + 2
                def exps(a, s):
                    for ib in range(TB):
                        w = prob1[:, nxt.base % 2, s, a, ib, ib * (TOK - WIN):ib * (TOK - WIN) + WIN]
                        wait(act, min_done[1], nxt.times(4 * HP, 4 * s + 2 * a + ib + 1))
                        act.activation(w, w, ACT.Exp, bias=row_min1[:, nxt.base % 2, s, a, ib:ib + 1], scale=-1.0,
                                       accum_out=row_sum1[:, nxt.base % 2, s, a, ib:ib + 1]).then_inc(exp_done[1], 1)

                for s in range(HP):
                    if s == 0 and nxt.exists:
                        wait(act, k_ps[1], nxt.times(1, 1))
                        for hp in range(HP):
                            act.activation(kT[:, nxt.base % 2, HIGH, hp], work[:, 1, hp], ACT.Identity,
                                           bias=vec1_sb[:, 1, hp:hp + 1]).then_inc(k_high[1], 1)
                    if m.exists:
                        wait(act, turn_ps[1][0], m.times(HP, s + 1))
                        wait(act, mix_ps[1], m.times(HP, s + 1 - HP))
                        act.copy(probT1[:, s, 0], turn[:, SPAN]).then_inc(turn_done[1][0], 1)
                    if s == 0 and last.exists:
                        wait(act, mix_ps[1], last.times(HP, HP))
                        wait(act, y_ps[1], last.times(1, 0))
                        act.copy(att[:, HIGH], mix[:]).then_inc(att_high[1], 1)
                    if s == 1 and far.exists:
                        wait(act, q_ps[1], far.times(1, 1))
                        for hp in range(HP):
                            act.activation(nqT[:, far.base % 2, HIGH, hp], work[:, 0, hp], ACT.Identity,
                                           bias=b_q1[:, hp:hp + 1]).then_inc(q_high[1], 1)
                    if nxt.exists:
                        exps(0, s)
                        exps(1, s)

            over_rows(act, 2, 1, body1)

        @block.vector
        def _(dve):
            dve.wait_ge(consts_in, 16 * 11)
            dve.tensor_scalar(half_gate_b[:], vec0_sb[:, 2], 0.5, None, ALU.mult).then_inc(consts_set, 1)
            dve.tensor_scalar(b_q1[:], vec1_sb[:, 0], -float(D1) ** -0.5, None, ALU.mult)
            n = 0
            for w, w_in, scales in weights:
                for cols, scale in scales:
                    n += 1
                    dve.wait_ge(high_set, n)
                    dve.scalar_tensor_tensor(out=w[:, LOW, :, cols], in0=w_in[:, :, cols], scalar=scale,
                                             in1=w[:, HIGH, :, cols].bitcast(F32), op0=ALU.mult, op1=ALU.subtract
                                             ).then_inc(weights_set, 1)
            dve.wait_ge(consts_set, 2)

            def chunks(plus, more):
                for b in range(2):
                    wait(dve, x_chunk_in[b], plus(16, 16))
                    apart(dve, dve_passed)
                    for cb in range(CB):
                        for t in range(XCHUNK // 512):
                            at = bass.ds(plus(2 * XCHUNK // 512, b * (XCHUNK // 512) + t), 1)
                            dve.bn_stats(gstat0[:, cb, at], x_chunk[:, b, cb, t * 512:(t + 1) * 512]
                                         ).then_inc(x_chunk_used, 1)
                    wait(dve, bias_turned, plus(2, b + 1))
                    apart(dve, dve_passed)
                    keys = bass.ds(plus(2 * JCHUNK, b * JCHUNK), JCHUNK)
                    for ib in range(TB):
                        dve.tensor_copy(neg_bias[:, ib, :, keys].rearrange("p h (q k) -> p k q h", k=2),
                                        score[:, 2 + b, :, ib * P:(ib + 1) * P].rearrange("p k (q n) -> p k q n", n=QUAD)
                                        [:, :, :, 0:H0]).then_inc(bias_done, 1)

            over_chunks(dve, NXC, chunks)

            def group_norm(n, stat):
                for cb in range(CB):
                    dve.bn_aggr(ch_mv[:, cb], stat[:, cb].rearrange("p n s -> p (n s)")).then_inc(gn_chain[n], 1)
                dve.wait_ge(gn_ps[n], 1)
                dve.tensor_copy(gn_mean[:], mix[:, 0, 0:CB]).then_inc(gn_chain[n], 1)
                dve.wait_ge(gn_chain[n], 3)
                dve.tensor_tensor(gn_dev[:], ch_mv[:, :, 0], gn_mean[:], ALU.subtract).then_inc(gn_chain[n], 1)
                dve.wait_ge(gn_chain[n], 4)
                dve.tensor_tensor(gn_sq[:], gn_dev[:], gn_dev[:], ALU.mult).then_inc(gn_chain[n], 1)
                dve.wait_ge(gn_chain[n], 5)
                dve.tensor_tensor(gn_sq[:], gn_sq[:], ch_mv[:, :, 1], ALU.add).then_inc(gn_chain[n], 1)
                dve.wait_ge(gn_ps[n], 2)
                dve.tensor_scalar(gn_var[:], mix[:, 0, CB:2 * CB], EPS, None, ALU.add).then_inc(gn_chain[n], 1)
                dve.wait_ge(gn_rstd[n], 1)
                dve.scalar_tensor_tensor(out=gn_shift[n][:], in0=gn_mean[:], scalar=-1.0, in1=gn_scale[n][:],
                                         op0=ALU.mult, op1=ALU.mult).then_inc(gn_ready[n], 1)

            dve.wait_ge(x_chunk_used, XSTATS * NXC)
            group_norm(0, gstat0)
            dve.wait_ge(gn_ready[0], 1)
            for n, of in enumerate((gn_scale[0], gn_shift[0])):
                for cb in range(CB):
                    dve.tensor_scalar(gn_diag[:, n, cb], ident[:], of[:, cb:cb + 1], None, ALU.mult).then_inc(gn_diag_set, 1)
            dve.wait_ge(gn_row_ps, 1)
            dve.tensor_copy(gn_row[:].rearrange("p n c -> p (n c)"), turn[:]).then_inc(gn_row_done, 1)
            dve.wait_ge(bias_done, TB * NJC)

            def split(n, m, x):
                dve.tensor_copy(src[:, m.base % 2, HIGH], x).then_inc(src_high[n], 1)
                wait(dve, src_high[n], m.times(1, 1))
                dve.tensor_tensor(src[:, m.base % 2, LOW], x, src[:, m.base % 2, HIGH].bitcast(F32), ALU.subtract
                                  ).then_inc(src_done[n], 1)

            def residual(n, last, bank, bias):
                wait(dve, y_ps[n], last.times(1, 1))
                wait(dve, y_out[n][last.base % 2], last.times(16, 0, of=2))
                if n == 0:
                    wait(dve, x_in[n][last.base % XSLOTS], last.times(16, 16, of=XSLOTS))
                    apart(dve, dve_passed)
                for ob in range(CB):
                    dve.scalar_tensor_tensor(out=y_sb[:, last.base % 2, ob], in0=work[:, bank, ob], scalar=bias[:, ob:ob + 1],
                                             in1=x_sb[:, last.base % XSLOTS, ob], op0=ALU.add, op1=ALU.add
                                             ).then_inc(y_done[n], 1)

            def body0(m):
                last, nxt, far = m + -1, m + 1, m + 2

                def mins(r, g, a):
                    wait(dve, score_done[0], r.times(2 * STEPS0, 2 * g + a + 1))
                    wait(dve, turn_ps[0][a], r.times(STEPS0, g + 1 - STEPS0))
                    apart(dve, dve_passed)
                    for ib in range(TB):
                        dve.tensor_tensor_reduce(prob[:, g, a, ib], score[:, (2 * g + a) % HPG, ib],
                                                 neg_bias[:, ib, 2 * g + a], 1.0, 3.0e38, ALU.add, ALU.min,
                                                 row_min[:, g, a, ib:ib + 1]).then_inc(min_done[0], 1)

                for s in range(STEPS0):
                    if s == 1 and nxt.exists:
                        wait(dve, k_high[0], nxt.times(1, 1))
                        dve.tensor_tensor(kT[:, nxt.base % 2, LOW], work[:, 1],
                                          kT[:, nxt.base % 2, HIGH].bitcast(F32), ALU.subtract).then_inc(k_done[0], 1)
                    r, g = (m, s + 1) if s + 1 < STEPS0 else (nxt, 0)
                    if r.exists:
                        wait(dve, exp_done[0], r.times(4 * STEPS0, 4 * (g + 1)))
                        dve.reciprocal(row_inv[:, g], row_sum[:, g]).then_inc(inv_done[0], 1)
                    if s == 3 and last.exists:
                        residual(0, last, 1, vec0_sb[:, 3])
                        for ob in range(CB):
                            wait(dve, y_done[0], last.times(CB, ob + 1))
                            apart(dve, dve_passed)
                            at = slice(last.base, last.base + 1) if last.loop is None else bass.ds(last.times(1), 1)
                            dve.bn_stats(gstat1[:, ob, at], y_sb[:, last.base % 2, ob]).then_inc(y_stats, 1)
                    r, g = (m, s + 2) if s < 2 else (nxt, s - 2)
                    if r.exists:
                        mins(r, g, 0)
                    if s == 0 and last.exists:
                        wait(dve, mix_ps[0], last.times(STEPS0, STEPS0))
                        wait(dve, gate_done, last.times(HG, HG))
                        wait(dve, att_done[0], last.times(1, 0))
                        dve.scalar_tensor_tensor(out=att_sum[:], in0=gate[:, last.base % 2], scalar=1.0, in1=mix[:],
                                                 op0=ALU.add, op1=ALU.mult).then_inc(att_sum_done, 1)
                    if s == 1 and last.exists:
                        wait(dve, att_high[0], last.times(1, 1))
                        dve.tensor_tensor(att[:, LOW], att_sum[:], att[:, HIGH].bitcast(F32), ALU.subtract
                                          ).then_inc(att_done[0], 1)
                    if s == 2 and far.exists:
                        wait(dve, ln_rstd_done, far.times(1, 1))
                        wait(dve, t2_done, far.times(1, 0))
                        for tb in range(TB):
                            dve.tensor_scalar(xn[:, tb], g_tok[:, far.base % 2, tb], ln_mv[:, tb, 0:1],
                                              ln_rstd[:, tb:tb + 1], ALU.subtract, ALU.mult).then_inc(xn_done, 1)
                    if r.exists:
                        mins(r, g, 1)
                    if s == 3 and far.exists:
                        wait(dve, xnT_done, far.times(CB, CB))
                        wait(dve, gate_ps, far.times(1, -1))
                        split(0, far, xnT[:])
                    if m.exists:
                        wait(dve, turn_ps[0][1], m.times(STEPS0, s + 1))
                        wait(dve, mix_ps[0], m.times(STEPS0, s - 1))
                        dve.tensor_copy(probT[:, s % 2, 1], turn[:]).then_inc(turn_done[0][1], 1)
                    if s == 0 and nxt.exists:
                        wait(dve, q_high[0], nxt.times(1, 1))
                        dve.tensor_tensor(nqT[:, nxt.base % 2, LOW], work[:, 0],
                                          nqT[:, nxt.base % 2, HIGH].bitcast(F32), ALU.subtract).then_inc(q_done[0], 1)
                    if s == 1 and far.exists:
                        wait(dve, g_done[0], far.times(1, 1))
                        apart(dve, dve_passed)
                        for tb in range(TB):
                            dve.bn_stats(ln_st[:, tb], g_tok[:, far.base % 2, tb]).then_inc(ln_chain, 1)
                        for tb in range(TB):
                            wait(dve, ln_chain, far.times(2 * TB, tb + 1))
                            apart(dve, dve_passed)
                            dve.bn_aggr(ln_mv[:, tb], ln_st[:, tb]).then_inc(ln_chain, 1)
                        wait(dve, ln_chain, far.times(2 * TB, 2 * TB))
                        dve.tensor_scalar(ln_var[:], ln_mv[:, :, 1], EPS, None, ALU.add).then_inc(ln_var_done, 1)

            over_rows(dve, 2, 1, body0)

            dve.wait_ge(y_stats, CB * ROWS)
            group_norm(1, gstat1)
            dve.wait_ge(prob1_clear, 1)

            def body1(m):
                last, nxt, far = m + -1, m + 1, m + 2

                def mins(a, s):
                    wait(dve, score_done[1], nxt.times(2 * HP, 2 * s + a + 1))
                    wait(dve, turn_ps[1][a], nxt.times(HP, s + 1 - 2 * HP))
                    apart(dve, dve_passed)
                    for ib in range(TB):
                        j0 = ib * (TOK - WIN)
                        dve.tensor_tensor_reduce(prob1[:, nxt.base % 2, s, a, ib, j0:j0 + WIN],
                                                 score[:, 2 * s + a, ib, 0:WIN], band[:, ib], 1.0, 3.0e38,
                                                 ALU.add, ALU.min, row_min1[:, nxt.base % 2, s, a, ib:ib + 1]
                                                 ).then_inc(min_done[1], 1)

                def low(r, to, at, bias, done):
                    for hp in range(HP):
                        dve.scalar_tensor_tensor(out=to[:, r.base % 2, LOW, hp], in0=work[:, at, hp],
                                                 scalar=bias[:, hp:hp + 1], in1=to[:, r.base % 2, HIGH, hp].bitcast(F32),
                                                 op0=ALU.add, op1=ALU.subtract).then_inc(done, 1)

                for s in range(HP):
                    if s == 0 and nxt.exists:
                        wait(dve, k_high[1], nxt.times(HP, HP))
                        low(nxt, kT, 1, vec1_sb[:, 1], k_done[1])
                    if s == 1 and last.exists:
                        residual(1, last, 1, vec1_sb[:, 2])
                    r, g = (m, 1) if s == 0 else (nxt, 0)
                    if r.exists:
                        wait(dve, exp_done[1], r.times(4 * HP, 4 * (g + 1)))
                        dve.reciprocal(row_inv1[:, r.base % 2, g], row_sum1[:, r.base % 2, g]).then_inc(inv_done[1], 1)
                    if s == 0 and nxt.exists:
                        wait(dve, v_ps[1], nxt.times(1, 1))
                        dve.tensor_tensor(v_sb[:, nxt.base % 4], work[:, 0], bv1_sb[:].unsqueeze(1).broadcast_to([P, TB, CH]),
                                          ALU.add).then_inc(v_done[1], 1)
                    if s == 0 and last.exists:
                        wait(dve, att_high[1], last.times(1, 1))
                        dve.tensor_tensor(att[:, LOW], mix[:], att[:, HIGH].bitcast(F32), ALU.subtract
                                          ).then_inc(att_done[1], 1)
                    if m.exists:
                        wait(dve, turn_ps[1][1], m.times(HP, s + 1))
                        wait(dve, mix_ps[1], m.times(HP, s + 1 - HP))
                        dve.tensor_copy(probT1[:, s, 1], turn[:, SPAN]).then_inc(turn_done[1][1], 1)
                    if nxt.exists:
                        mins(0, s)
                        mins(1, s)
                    if s == 0 and far.exists:
                        wait(dve, g_done[1], far.times(1, 1))
                        wait(dve, v_ps[1], far.times(1, -1))
                        split(1, far, g_sb[:, far.base % 2])
                    if s == 1 and far.exists:
                        wait(dve, q_high[1], far.times(HP, HP))
                        low(far, nqT, 0, b_q1, q_done[1])

            over_rows(dve, 2, 1, body1)


def channels(v):
    return np.asarray(v).reshape(CB, P).T


def rows_first(w, cols):
    return np.ascontiguousarray(np.asarray(w).reshape(CB, P, cols).transpose(1, 0, 2))


def kernel(**inputs):
    import concourse.bacc as bacc
    from concourse.bass_utils import run_bass_kernel_spmd

    a = {k: np.asarray(v) for k, v in inputs.items()}
    xT = np.ascontiguousarray(a["x"][0].transpose(2, 0, 1)).reshape(CH, ROWS * TOK)
    pairT = np.ascontiguousarray(a["L0_conv_x2d"][0].transpose(2, 1, 0))
    qkv = a["L0_conv_qkv_w"].reshape(D0, 3, H0, CH).transpose(3, 1, 2, 0).reshape(CH, 3 * CH)
    gate = a["L0_conv_gate_w"].reshape(D0, H0, CH).transpose(2, 1, 0).reshape(CH, CH)
    gate_b = a["L0_conv_gate_b"].reshape(D0, H0).T.reshape(CH)
    final = a["L0_conv_final_w"].T.reshape(D0, H0, CH).transpose(1, 0, 2).reshape(CH, CH)
    b_in = a["L1_conv_b_in"]

    c = np.arange(P)
    group_mean = np.where(c[:, None] // GROUP == c[None, :] // GROUP, 1.0 / GROUP, 0.0).astype(np.float32)
    queries = c[:, None, None] + P * np.arange(TB)[None, :, None]
    keys = np.arange(WIN)[None, None, :] + (TOK - WIN) * np.arange(TB)[None, :, None]
    band = np.where(abs(queries - keys) <= BAND, 0.0, FAR).astype(np.float32)

    arrays = {
        "xT": xT,
        "x_nat": np.ascontiguousarray(a["x"][0].reshape(ROWS * TOK, CH)),
        "pairT": pairT,
        "w0_d": rows_first(np.concatenate([qkv, gate], axis=1), 4 * CH),
        "wf0_d": rows_first(final, CH),
        "pair_w": np.ascontiguousarray(a["L0_conv_x2d_w"].T),
        "vec0": np.ascontiguousarray(np.stack([channels(v) for v in (
            a["L0_conv_norm_w"], a["L0_conv_norm_b"], gate_b, a["L0_conv_final_b"])], axis=1)),
        "w1_d": rows_first(a["L1_conv_w_in"].T, 3 * CH),
        "wf1_d": rows_first(a["L1_conv_w_out"].T, CH),
        "vec1": np.ascontiguousarray(np.stack([channels(v) for v in (
            b_in[:CH], b_in[CH:2 * CH], a["L1_conv_b_out"])], axis=1)),
        "bv1": np.ascontiguousarray(b_in[2 * CH:].reshape(1, CH)),
        "ident_d": np.eye(P, dtype=np.float32),
        "group_d": group_mean,
        "band_d": band,
    }
    nc = bacc.Bacc("TRN2", target_bir_lowering=False, num_devices=1)
    aps = {n: nc.dram_tensor(n, v.shape, F32, kind="ExternalInput").ap() for n, v in arrays.items()}
    aps["x1T"] = nc.dram_tensor("x1T", (CH, ROWS * TOK), F32, kind="Internal").ap()
    aps["outT"] = nc.dram_tensor("outT", (CH, ROWS * TOK), F32, kind="ExternalOutput").ap()
    conv_preact_kernel(nc, **aps)
    r = run_bass_kernel_spmd(nc, [arrays], core_ids=[0])
    out = r.results[0]["outT"].reshape(CH, ROWS, TOK).transpose(1, 2, 0)
    return np.ascontiguousarray(out).reshape(1, ROWS, TOK, CH)
```
